# Optimizing a Trainium2 kernel written in Bass

```python
import numpy as np
import jax
import jax.numpy as jnp

def _softmax(x, axis=-1):
    return jax.nn.softmax(x, axis=axis)

def _gelu(x):
    return jax.nn.gelu(x, approximate=True)

def _silu(x):
    return jax.nn.silu(x)

def _sigmoid(x):
    return jax.nn.sigmoid(x)

def _layernorm(x, axis=-1, eps=1e-05):
    m = jnp.mean(x, axis=axis, keepdims=True)
    v = jnp.var(x, axis=axis, keepdims=True)
    return (x - m) / jnp.sqrt(v + eps)

def _scatter_add(tgt, idx, src, axis=0):
    return tgt.at[idx].add(src)

def _segment_sum(src, seg, n):
    return jax.ops.segment_sum(src, seg, n)
kernel_name = 'mk_hybrid_d2_jaxref_r8_6018f7'

def setup_inputs(seed: int=0):
    np.random.seed(seed)
    _w = jnp.asarray

    def _L0_attn_a_setup():
        import jax, jax.numpy as jnp
        import numpy as np
        D_MODEL = 128
        NUM_HEADS = 16
        D_HEAD = D_MODEL // NUM_HEADS
        PATCH = 128

        def _patched_attn(x, Wq, bq, Wk, bk, Wv, bv, Wo, bo):
            B, T, D = x.shape
            P = PATCH
            pad_len = (P - T % P) % P
            if pad_len > 0:
                x = jnp.pad(x, ((0, 0), (0, pad_len), (0, 0)))
            Tp = T + pad_len
            n = Tp // P
            xp = x.reshape(B * n, P, D)

            def heads(y):
                return y.reshape(B * n, P, NUM_HEADS, D_HEAD).transpose(0, 2, 1, 3)
            q = heads(xp @ Wq + bq)
            k = heads(xp @ Wk + bk)
            v = heads(xp @ Wv + bv)
            scores = jnp.einsum('bhtd,bhTd->bhtT', q, k) / jnp.sqrt(jnp.asarray(D_HEAD, x.dtype))
            w = jax.nn.softmax(scores, axis=-1)
            out = jnp.einsum('bhtT,bhTd->bhtd', w, v)
            out = out.transpose(0, 2, 1, 3).reshape(B * n, P, D)
            out = out @ Wo + bo
            out = out.reshape(B, Tp, D)
            if pad_len > 0:
                out = out[:, :T, :]
            return out
        key = jax.random.key(seed)
        ks = jax.random.split(key, 10)
        B, T = (4, 1024)
        x = jax.random.normal(ks[0], (B, T, D_MODEL), dtype=jnp.float32)
        coords = jax.random.uniform(ks[1], (B, T, 2), dtype=jnp.float32)
        s = 1.0 / np.sqrt(D_MODEL)
        Wq = jax.random.normal(ks[2], (D_MODEL, D_MODEL), dtype=jnp.float32) * s
        Wk = jax.random.normal(ks[3], (D_MODEL, D_MODEL), dtype=jnp.float32) * s
        Wv = jax.random.normal(ks[4], (D_MODEL, D_MODEL), dtype=jnp.float32) * s
        Wo = jax.random.normal(ks[5], (D_MODEL, D_MODEL), dtype=jnp.float32) * s
        bq = jnp.zeros((D_MODEL,), jnp.float32)
        bk = jnp.zeros((D_MODEL,), jnp.float32)
        bv = jnp.zeros((D_MODEL,), jnp.float32)
        bo = jnp.zeros((D_MODEL,), jnp.float32)
        return {'x': x, 'coords': coords, 'Wq': Wq, 'bq': bq, 'Wk': Wk, 'bk': bk, 'Wv': Wv, 'bv': bv, 'Wo': Wo, 'bo': bo}
    _L0_attn_a_in = _L0_attn_a_setup()

    def _L0_attn_b_setup():
        import jax, jax.numpy as jnp
        import numpy as np
        B, S, D_IN = (2, 256, 128)
        H, D_HEAD = (16, 64)
        key = jax.random.key(seed)
        k1, k2, k3 = jax.random.split(key, 3)
        x = jax.random.normal(k1, (B, S, D_IN), dtype=jnp.float32)
        kernel = jax.random.normal(k2, (3, H, D_IN, D_HEAD), dtype=jnp.float32) * np.float32(np.sqrt(2.0 / D_IN))
        WO = jax.random.normal(k3, (1, H * D_HEAD, D_IN), dtype=jnp.float32) * np.float32(np.sqrt(2.0 / (H * D_HEAD)))
        return {'x': x, 'kernel': kernel, 'WO': WO}
    _L0_attn_b_in = _L0_attn_b_setup()

    def _L0_ffn_setup():
        import jax, jax.numpy as jnp
        import numpy as np
        B, T, D = (2, 256, 128)
        DCD = 512
        RET = 128
        NEXP = 512
        NKEYS = 64
        H = 4
        KPH = 8
        key = jax.random.key(seed)
        ks = jax.random.split(key, 10)
        s = lambda k, shape, scale: jax.random.normal(k, shape, jnp.float32) * scale
        return {'hidden_states': jax.random.normal(ks[0], (B, T, D), jnp.float32), 'Wg': s(ks[1], (D, DCD), 0.02), 'bg': jnp.zeros((DCD,), jnp.float32), 'Wu': s(ks[2], (D, DCD), 0.02), 'bu': jnp.zeros((DCD,), jnp.float32), 'Wd': s(ks[3], (DCD, D), 0.02), 'bd': jnp.zeros((D,), jnp.float32), 'Wq': s(ks[4], (D, RET * H), 0.02), 'keys': s(ks[5], (H, NKEYS, 2, RET // 2), 0.02), 'down_embed': s(ks[6], (NEXP, D), 0.02), 'up_embed': s(ks[7], (NEXP, D), 0.02)}
    _L0_ffn_in = _L0_ffn_setup()

    def _L1_attn_a_setup():
        import jax, jax.numpy as jnp
        import numpy as np
        HIDDEN = 128
        HEADS = 16
        HEAD_DIM = HIDDEN // HEADS
        SCALE = HEAD_DIM ** (-0.5)
        key = jax.random.key(seed)
        ks = jax.random.split(key, 9)
        init = 1.0 / np.sqrt(HIDDEN)
        hidden_states = jax.random.normal(ks[0], (8, 128, HIDDEN), dtype=jnp.float32)

        def lin(k):
            kw, kb = jax.random.split(k)
            W = jax.random.uniform(kw, (HIDDEN, HIDDEN), jnp.float32, -init, init)
            b = jax.random.uniform(kb, (HIDDEN,), jnp.float32, -init, init)
            return (W, b)
        Wq, bq = lin(ks[1])
        Wk, bk = lin(ks[2])
        Wv, bv = lin(ks[3])
        Wo, bo = lin(ks[4])
        return {'hidden_states': hidden_states, 'Wq': Wq, 'bq': bq, 'Wk': Wk, 'bk': bk, 'Wv': Wv, 'bv': bv, 'Wo': Wo, 'bo': bo}
    _L1_attn_a_in = _L1_attn_a_setup()

    def _L1_attn_b_setup():
        import jax, jax.numpy as jnp
        import numpy as np
        import math
        FEATURE_DIM = 128
        NUM_HEADS = 16
        HEAD_SIZE = FEATURE_DIM // NUM_HEADS
        key = jax.random.key(seed)
        ks = jax.random.split(key, 5)
        B, T, C = (4, 256, FEATURE_DIM)
        scale = 1.0 / math.sqrt(C)
        x = jax.random.normal(ks[0], (B, T, C), dtype=jnp.float32)
        W_qkv = jax.random.uniform(ks[1], (3 * C, C), jnp.float32, -scale, scale)
        b_qkv = jax.random.uniform(ks[2], (3 * C,), jnp.float32, -scale, scale)
        W_out = jax.random.uniform(ks[3], (C, C), jnp.float32, -scale, scale)
        b_out = jax.random.uniform(ks[4], (C,), jnp.float32, -scale, scale)
        return {'x': x, 'W_qkv': W_qkv, 'b_qkv': b_qkv, 'W_out': W_out, 'b_out': b_out}
    _L1_attn_b_in = _L1_attn_b_setup()

    def _L1_ffn_setup():
        import jax, jax.numpy as jnp
        import numpy as np
        NUM_GEMMS = 8
        HIDDEN = 128
        INTER = 512
        key = jax.random.key(seed)
        k_x, k_w1, k_b1, k_w2, k_b2 = jax.random.split(key, 5)
        x = jax.random.normal(k_x, (8, 256, HIDDEN), dtype=jnp.float32)
        s1 = 1.0 / np.sqrt(HIDDEN)
        s2 = 1.0 / np.sqrt(INTER)
        W1 = jax.random.uniform(k_w1, (NUM_GEMMS, INTER, HIDDEN), jnp.float32, -s1, s1)
        b1 = jax.random.uniform(k_b1, (NUM_GEMMS, INTER), jnp.float32, -s1, s1)
        W2 = jax.random.uniform(k_w2, (NUM_GEMMS, HIDDEN, INTER), jnp.float32, -s2, s2)
        b2 = jax.random.uniform(k_b2, (NUM_GEMMS, HIDDEN), jnp.float32, -s2, s2)
        return {'x': x, 'W1': W1, 'b1': b1, 'W2': W2, 'b2': b2}
    _L1_ffn_in = _L1_ffn_setup()
    _d = {'L0_attn_a_x': _L0_attn_a_in['x'], 'L0_attn_a_coords': _L0_attn_a_in['coords'], 'L0_attn_a_Wq': _L0_attn_a_in['Wq'], 'L0_attn_a_bq': _L0_attn_a_in['bq'], 'L0_attn_a_Wk': _L0_attn_a_in['Wk'], 'L0_attn_a_bk': _L0_attn_a_in['bk'], 'L0_attn_a_Wv': _L0_attn_a_in['Wv'], 'L0_attn_a_bv': _L0_attn_a_in['bv'], 'L0_attn_a_Wo': _L0_attn_a_in['Wo'], 'L0_attn_a_bo': _L0_attn_a_in['bo'], 'L0_attn_b_kernel': _L0_attn_b_in['kernel'], 'L0_attn_b_WO': _L0_attn_b_in['WO'], 'L0_ffn_Wg': _L0_ffn_in['Wg'], 'L0_ffn_bg': _L0_ffn_in['bg'], 'L0_ffn_Wu': _L0_ffn_in['Wu'], 'L0_ffn_bu': _L0_ffn_in['bu'], 'L0_ffn_Wd': _L0_ffn_in['Wd'], 'L0_ffn_bd': _L0_ffn_in['bd'], 'L0_ffn_Wq': _L0_ffn_in['Wq'], 'L0_ffn_keys': _L0_ffn_in['keys'], 'L0_ffn_down_embed': _L0_ffn_in['down_embed'], 'L0_ffn_up_embed': _L0_ffn_in['up_embed'], 'L1_attn_a_Wq': _L1_attn_a_in['Wq'], 'L1_attn_a_bq': _L1_attn_a_in['bq'], 'L1_attn_a_Wk': _L1_attn_a_in['Wk'], 'L1_attn_a_bk': _L1_attn_a_in['bk'], 'L1_attn_a_Wv': _L1_attn_a_in['Wv'], 'L1_attn_a_bv': _L1_attn_a_in['bv'], 'L1_attn_a_Wo': _L1_attn_a_in['Wo'], 'L1_attn_a_bo': _L1_attn_a_in['bo'], 'L1_attn_b_W_qkv': _L1_attn_b_in['W_qkv'], 'L1_attn_b_b_qkv': _L1_attn_b_in['b_qkv'], 'L1_attn_b_W_out': _L1_attn_b_in['W_out'], 'L1_attn_b_b_out': _L1_attn_b_in['b_out'], 'L1_ffn_W1': _L1_ffn_in['W1'], 'L1_ffn_b1': _L1_ffn_in['b1'], 'L1_ffn_W2': _L1_ffn_in['W2'], 'L1_ffn_b2': _L1_ffn_in['b2']}
    _x0 = _d['L0_attn_a_x']
    _d['L0_attn_a_x'] = jax.random.normal(jax.random.fold_in(jax.random.key(seed), 1), (8, 512, 128), dtype=_x0.dtype)
    del _x0
    return _d

def reference(L0_attn_a_x, L0_attn_a_coords, L0_attn_a_Wq, L0_attn_a_bq, L0_attn_a_Wk, L0_attn_a_bk, L0_attn_a_Wv, L0_attn_a_bv, L0_attn_a_Wo, L0_attn_a_bo, L0_attn_b_kernel, L0_attn_b_WO, L0_ffn_Wg, L0_ffn_bg, L0_ffn_Wu, L0_ffn_bu, L0_ffn_Wd, L0_ffn_bd, L0_ffn_Wq, L0_ffn_keys, L0_ffn_down_embed, L0_ffn_up_embed, L1_attn_a_Wq, L1_attn_a_bq, L1_attn_a_Wk, L1_attn_a_bk, L1_attn_a_Wv, L1_attn_a_bv, L1_attn_a_Wo, L1_attn_a_bo, L1_attn_b_W_qkv, L1_attn_b_b_qkv, L1_attn_b_W_out, L1_attn_b_b_out, L1_ffn_W1, L1_ffn_b1, L1_ffn_W2, L1_ffn_b2):

    def _L0_attn_a_ref(x, coords, Wq, bq, Wk, bk, Wv, bv, Wo, bo):
        import jax, jax.numpy as jnp
        import numpy as np
        D_MODEL = 128
        NUM_HEADS = 16
        D_HEAD = D_MODEL // NUM_HEADS
        PATCH = 128

        def _patched_attn(x, Wq, bq, Wk, bk, Wv, bv, Wo, bo):
            B, T, D = x.shape
            P = PATCH
            pad_len = (P - T % P) % P
            if pad_len > 0:
                x = jnp.pad(x, ((0, 0), (0, pad_len), (0, 0)))
            Tp = T + pad_len
            n = Tp // P
            xp = x.reshape(B * n, P, D)

            def heads(y):
                return y.reshape(B * n, P, NUM_HEADS, D_HEAD).transpose(0, 2, 1, 3)
            q = heads(xp @ Wq + bq)
            k = heads(xp @ Wk + bk)
            v = heads(xp @ Wv + bv)
            scores = jnp.einsum('bhtd,bhTd->bhtT', q, k) / jnp.sqrt(jnp.asarray(D_HEAD, x.dtype))
            w = jax.nn.softmax(scores, axis=-1)
            out = jnp.einsum('bhtT,bhTd->bhtd', w, v)
            out = out.transpose(0, 2, 1, 3).reshape(B * n, P, D)
            out = out @ Wo + bo
            out = out.reshape(B, Tp, D)
            if pad_len > 0:
                out = out[:, :T, :]
            return out
        return _patched_attn(x, Wq, bq, Wk, bk, Wv, bv, Wo, bo)

    def _L0_attn_b_ref(x, kernel, WO):
        import jax, jax.numpy as jnp
        import numpy as np
        B, S, D_IN = (2, 256, 128)
        H, D_HEAD = (16, 64)
        b, s, _ = x.shape
        h, d = (kernel.shape[1], kernel.shape[3])
        q = jnp.einsum('bsm,hmd->bhsd', x, kernel[0])
        k = jnp.einsum('bsm,hmd->bhsd', x, kernel[1])
        v = jnp.einsum('bsm,hmd->bhsd', x, kernel[2])
        scale = jnp.float32(1.0 / (d * d * h))
        scores = jnp.einsum('bhsd,bhtd->bhst', q, k) * scale
        attn = jax.nn.softmax(scores, axis=-1)
        out = jnp.einsum('bhst,bhtd->bhsd', attn, v)
        out = jnp.transpose(out, (0, 2, 3, 1)).reshape(b, s, d * h)
        out = jnp.einsum('bsf,fm->bsm', out, WO[0])
        return out

    def _L0_ffn_ref(hidden_states, Wg, bg, Wu, bu, Wd, bd, Wq, keys, down_embed, up_embed):
        import jax, jax.numpy as jnp
        import numpy as np
        B, T, D = (2, 256, 128)
        DCD = 512
        RET = 128
        NEXP = 512
        NKEYS = 64
        H = 4
        KPH = 8
        b, t, d = hidden_states.shape
        q = (hidden_states @ Wq).reshape(b, t, 2, H, RET // 2)
        sim = jnp.einsum('btphn,hkpn->pbthk', q, keys)
        sc, ix = jax.lax.top_k(sim, KPH)
        sx, sy = (sc[0], sc[1])
        ixx, ixy = (ix[0], ix[1])
        all_sc = (sx[..., :, None] + sy[..., None, :]).reshape(b, t, H, KPH * KPH)
        all_ix = (ixx[..., :, None] * NKEYS + ixy[..., None, :]).reshape(b, t, H, KPH * KPH)
        scores, pk = jax.lax.top_k(all_sc, KPH)
        idx = jnp.take_along_axis(all_ix, pk, axis=-1)
        de = down_embed[idx]
        ue = up_embed[idx]
        w = jnp.einsum('btd,bthkd->bthk', hidden_states, de)
        w = jax.nn.silu(w) * jax.nn.softmax(scores, axis=-1)
        experts_states = jnp.einsum('bthk,bthkd->btd', w, ue)
        mlp = jax.nn.silu(hidden_states @ Wg + bg) * (hidden_states @ Wu + bu) @ Wd + bd
        return mlp + experts_states

    def _L1_attn_a_ref(hidden_states, Wq, bq, Wk, bk, Wv, bv, Wo, bo):
        import jax, jax.numpy as jnp
        import numpy as np
        HIDDEN = 128
        HEADS = 16
        HEAD_DIM = HIDDEN // HEADS
        SCALE = HEAD_DIM ** (-0.5)
        b, s, d = hidden_states.shape
        q = (hidden_states @ Wq.T + bq).reshape(b, s, HEADS, HEAD_DIM)
        k = (hidden_states @ Wk.T + bk).reshape(b, s, HEADS, HEAD_DIM)
        v = (hidden_states @ Wv.T + bv).reshape(b, s, HEADS, HEAD_DIM)
        q = q * SCALE
        scores = jnp.einsum('bqhd,bkhd->bhqk', q, k)
        probs = jax.nn.softmax(scores.astype(jnp.float32), axis=-1).astype(scores.dtype)
        out = jnp.einsum('bhqk,bkhd->bqhd', probs, v).reshape(b, s, d)
        return out @ Wo.T + bo

    def _L1_attn_b_ref(x, W_qkv, b_qkv, W_out, b_out):
        import jax, jax.numpy as jnp
        import numpy as np
        import math
        FEATURE_DIM = 128
        NUM_HEADS = 16
        HEAD_SIZE = FEATURE_DIM // NUM_HEADS
        B, T, C = x.shape
        H, hs = (NUM_HEADS, HEAD_SIZE)
        qkv = x @ W_qkv.T + b_qkv
        qkv = qkv.reshape(B, T, H, 3 * hs)
        q = qkv[..., :hs]
        k = qkv[..., hs:2 * hs]
        v = qkv[..., 2 * hs:]
        att = jnp.einsum('bthd,bshd->bhts', q, k) / math.sqrt(hs)
        att_prob = jax.nn.softmax(att, axis=-1)
        att_v = jnp.einsum('bhts,bshd->bthd', att_prob, v)
        att_v = att_v.reshape(B, T, C)
        return att_v @ W_out.T + b_out

    def _L1_ffn_ref(x, W1, b1, W2, b2):
        import jax, jax.numpy as jnp
        import numpy as np
        NUM_GEMMS = 8
        HIDDEN = 128
        INTER = 512
        orig_shape = x.shape
        token_num = int(np.prod(orig_shape[:-1]))
        m = token_num // NUM_GEMMS
        xg = x.reshape(NUM_GEMMS, m, HIDDEN)
        h1 = jnp.einsum('gmh,goh->gmo', xg, W1) + b1[:, None, :]
        h2 = jnp.einsum('gmo,gho->gmh', h1, W2) + b2[:, None, :]
        return h2.reshape(orig_shape)
    x = L0_attn_a_x
    x = x + _L0_attn_a_ref(_layernorm(x, axis=-1), L0_attn_a_coords, L0_attn_a_Wq, L0_attn_a_bq, L0_attn_a_Wk, L0_attn_a_bk, L0_attn_a_Wv, L0_attn_a_bv, L0_attn_a_Wo, L0_attn_a_bo)
    x = x + _L0_ffn_ref(_layernorm(x, axis=-1), L0_ffn_Wg, L0_ffn_bg, L0_ffn_Wu, L0_ffn_bu, L0_ffn_Wd, L0_ffn_bd, L0_ffn_Wq, L0_ffn_keys, L0_ffn_down_embed, L0_ffn_up_embed)
    x = x + _L0_attn_b_ref(_layernorm(x, axis=-1), L0_attn_b_kernel, L0_attn_b_WO)
    x = x + _L0_ffn_ref(_layernorm(x, axis=-1), L0_ffn_Wg, L0_ffn_bg, L0_ffn_Wu, L0_ffn_bu, L0_ffn_Wd, L0_ffn_bd, L0_ffn_Wq, L0_ffn_keys, L0_ffn_down_embed, L0_ffn_up_embed)
    x = x + _L1_attn_a_ref(_layernorm(x, axis=-1), L1_attn_a_Wq, L1_attn_a_bq, L1_attn_a_Wk, L1_attn_a_bk, L1_attn_a_Wv, L1_attn_a_bv, L1_attn_a_Wo, L1_attn_a_bo)
    x = x + _L1_ffn_ref(_layernorm(x, axis=-1), L1_ffn_W1, L1_ffn_b1, L1_ffn_W2, L1_ffn_b2)
    x = x + _L1_attn_b_ref(_layernorm(x, axis=-1), L1_attn_b_W_qkv, L1_attn_b_b_qkv, L1_attn_b_W_out, L1_attn_b_b_out)
    x = x + _L1_ffn_ref(_layernorm(x, axis=-1), L1_ffn_W1, L1_ffn_b1, L1_ffn_W2, L1_ffn_b2)
    return x

_drawn_inputs = setup_inputs


def setup_inputs(seed=0):
    import zlib

    import numpy as np

    out = dict(_drawn_inputs(seed))
    spreads = {'L0_attn_a_bq': (0.0, 0.333),
     'L0_attn_a_bk': (0.0, 0.8),
     'L0_attn_a_bv': (0.0, 0.1),
     'L0_attn_a_bo': (0.0, 0.1),
     'L0_ffn_bg': (0.0, 0.633),
     'L0_ffn_bu': (0.0, 0.622),
     'L0_ffn_bd': (0.0, 0.1)}
    factors = {'L0_ffn_Wq': 8.0,
     'L0_ffn_keys': 8.0,
     'L0_ffn_down_embed': 4.156,
     'L0_ffn_up_embed': 4.58,
     'L1_attn_a_Wq': 6.693,
     'L1_attn_a_bq': 8.0,
     'L1_attn_a_Wk': 7.007,
     'L1_attn_a_bk': 8.0,
     'L1_attn_b_b_qkv': 2.888}
    for name, (base, spread) in spreads.items():
        noise = np.random.default_rng([zlib.crc32(name.encode()), seed]).standard_normal(out[name].shape)
        drawn = base * np.exp(spread * noise) if base else spread * noise
        out[name] = jnp.asarray(drawn.astype(out[name].dtype))
    for name, factor in factors.items():
        out[name] = (out[name] * factor).astype(out[name].dtype)
    return out
```

```python
from contextlib import ExitStack

import concourse.bass as bass
from concourse import mybir

F32 = mybir.dt.float32
F32R = mybir.dt.float32r
BF16 = mybir.dt.bfloat16
ALU = mybir.AluOpType
ACT = mybir.ActivationFunctionType
AX = mybir.AxisListType

P = 128
SEQS = 8
TILES = 4
SEQ = P * TILES
HEADS = 16
EPS = 1e-5


class Scope:

    def __init__(self, nc, ctx, stage, banks):
        self.nc, self.ctx, self.stage, self.banks, self.next_bank = nc, ctx, stage, banks, 0
        self.sems = []
        ctx.callback(self.clear)

    def sb(self, name, shape, dt=F32):
        return self.ctx.enter_context(self.nc.sbuf_tensor(f"{self.stage}_{name}", shape, dt))

    def ps(self, count=1):
        first = self.next_bank
        self.next_bank += count
        return self.banks[:, SEQ * first:SEQ * self.next_bank]

    def sem(self, name):
        self.sems.append(self.nc.alloc_semaphore(f"{self.stage}_{name}"))
        return self.sems[-1]

    def clear(self):
        self.nc.clear_and_free_semaphores(self.sems)
        self.nc.all_engine_barrier()


def over_sequences(eng, iteration):
    iteration(0, 0, "first")
    with eng.Fori(0, (SEQS - 2) // 2) as turn:
        iteration(turn * 2 + 1, 1, "middle")
        iteration(turn * 2 + 2, 0, "middle")
    iteration(SEQS - 1, 1, "last")
    iteration(SEQS, 0, "drain")


class Uses:

    def __init__(self, prologue, order):
        self.order = {k: order(k) for k in ("first", "middle", "last", "drain")}
        n = {k: len(v) for k, v in self.order.items()}
        self.prologue = prologue
        first = len(prologue)
        middle = first + n["first"]
        last = middle + (SEQS - 2) * n["middle"]
        self.per = n["middle"]
        self.base = {"first": first, "middle": middle, "last": last, "drain": last + n["last"]}

    def at(self, name, i=None, kind="prologue"):
        if kind == "prologue":
            return self.prologue.index(name)
        return self.number(self.order[kind].index(name), i, kind)

    def before(self, step, i, kind):
        return self.number(sum(name[0] < step for name in self.order[kind]), i, kind)

    def number(self, index, i, kind):
        n = self.base[kind] + index
        return (i - 1) * self.per + n if kind == "middle" else n


class NarrowWeights:

    LOADS = 8

    def __init__(self, nc, ctx, name, w, out_major):
        def sb(tile, shape):
            return ctx.enter_context(nc.sbuf_tensor(f"{name}_{tile}", shape, F32))
        self.w, self.out_major = w, out_major
        self.raw = {n: sb(f"raw_{n}", [P, P]) for n in "qkvo"}
        self.bq, self.bk, self.bv, self.bo = sb("bq", [P, 1]), sb("bk", [P, 1]), sb("bv", [P, P]), sb("bo", [P, P])
        self.loaded = ctx.enter_context(nc.semaphore(f"{name}_loaded"))

    def load(self, sp):
        for n in "qkvo":
            sp.dma_start(self.raw[n][:], self.w[n]).then_inc(self.loaded, 16)
        for tile, src in ((self.bv, self.w["bv"]), (self.bo, self.w["bo"])):
            sp.dma_start(tile[:], src.partition_broadcast(P)).then_inc(self.loaded, 16)
        for tile, src in ((self.bq, self.w["bq"]), (self.bk, self.w["bk"])):
            sp.dma_start(tile[:], src, allow_slow_non_contiguous=True).then_inc(self.loaded, 16)


def narrow_attention(nc, stage, x, ident, banks, weights, local, prefetch, rest_of_x=None):
    D = 8
    LEAD = 8
    GROUP = 4
    GROUPS = HEADS // GROUP
    PAIRS = 9
    KMAX = PAIRS * D
    KALL = KMAX + 2
    SLOTS = 2 * GROUP
    MAX_UNITS = 1 if local else TILES
    HEAD_COLS = SEQ if local else TILES * SEQ
    out_major = weights.out_major
    weights_in, N_LOADS = weights.loaded, weights.LOADS

    ctx = ExitStack()
    with ctx:
        s = Scope(nc, ctx, stage, banks)
        wq, wk, wv, wo = (s.sb(n, [P, P]) for n in ("wq", "wk", "wv", "wo"))
        raw, bq, bk, bv, bo = weights.raw, weights.bq, weights.bk, weights.bv, weights.bo
        minus_one = s.sb("minus_one", [2, SEQ], BF16)
        norms = Norms(s, x)
        xn = s.sb("xn", [P, TILES, P])
        xnT = s.sb("xnT", [P, SEQ])
        full = {n: s.sb(f"{n}_full", [P, SEQ]) for n in "qk"}
        rest = {n: s.sb(f"{n}_rest", [P, SEQ]) for n in "qk"}
        part = {n: [s.sb(f"{n}_part{j}", [P, SEQ], BF16) for j in range(3)] for n in "qk"}
        stackQ = s.sb("stackQ", [P, 2, HEADS, SEQ], BF16)
        stackK = s.sb("stackK", [P, 2, HEADS, SEQ], BF16)
        v_one = s.sb("v_one", [P, 2, TILES, HEADS, 32])
        rowmax = s.sb("rowmax", [P, 2, GROUP * TILES])
        maxT = s.sb("maxT", [GROUP * TILES, 2, 2, P], BF16)
        probs = s.sb("probs", [P, SLOTS, HEAD_COLS])
        outT = s.sb("outT", [P, 2, SEQ])
        rsum = s.sb("rsum", [P, TILES, GROUP])
        out = s.sb("out", [P, TILES, P])
        outT_all = s.sb("outT_all", [P, SEQ])
        ps_max = [s.ps() for j in range(2)]
        ps_exp = [s.ps(2) for j in range(2)]
        ps_pv = s.ps()
        ps_misc = s.ps()

        consts = s.sem("consts")
        ones_in = s.sem("ones_in")
        v_zero = s.sem("v_zero")
        w_ready = s.sem("w_ready")
        xn_done = s.sem("xn_done")
        bias_added = s.sem("bias_added")
        misc_full = s.sem("misc_full")
        misc_free = s.sem("misc_free")
        xnT_done = s.sem("xnT_done")
        full_done = {n: s.sem(f"{n}_full_done") for n in "qk"}
        part1_done = {n: s.sem(f"{n}_part1_done") for n in "qk"}
        rest_done = {n: s.sem(f"{n}_rest_done") for n in "qk"}
        part2_done = {n: s.sem(f"{n}_part2_done") for n in "qk"}
        part3_done = {n: s.sem(f"{n}_part3_done") for n in "qk"}
        rows_in = {n: s.sem(f"{n}_rows_in") for n in "qk"}
        v_done = s.sem("v_done")
        max_full = s.sem("max_full")
        max_done = s.sem("max_done")
        maxT1_done = s.sem("maxT1_done")
        maxT_done = s.sem("maxT_done")
        maxrows_in = s.sem("maxrows_in")
        exp_full = s.sem("exp_full")
        exp_done = s.sem("exp_done")
        pv_step = s.sem("pv_step")
        outT_done = s.sem("outT_done")
        rsum_done = s.sem("rsum_done")
        out_done = s.sem("out_done")
        outTall_done = s.sem("outTall_done")
        x_done = s.sem("x_done")

        def misc_uses(kind):
            main, nxt, before = kind != "drain", kind in ("first", "middle"), kind != "first"
            uses = []
            if main:
                uses.append((0, 1, "max1"))
            if before:
                uses.append((1, 1, "out2"))
            if nxt:
                uses += [(2, 0, "xnT"), (3, 0, "q"), (4, 0, "k")]
            if main:
                uses.append((4, 1, "max2"))
            if before:
                uses += [(5, 1, "out3"), (6, 1, "outT")]
            if nxt:
                uses.append((7, 0, "v"))
            if main:
                uses += [(8, 1, "max3"), (9, 1, "out0")]
            if before:
                uses.append((10, 1, "y"))
            if nxt:
                uses.append((12, 1, "max0"))
            if main:
                uses.append((13, 1, "out1"))
            return sorted(uses)

        prologue = (["w_q", "w_k", "w_v", "w_o"] if out_major else []) + ["xnT", "q", "k", "v", "max0"]
        misc = Uses(prologue, lambda k: [name for _, _, name in misc_uses(k)])
        tasks = {k: {(st, hf): name for st, hf, name in misc_uses(k)} for k in ("first", "middle", "last", "drain")}

        def max_now(kind, step):
            return kind in ("first", "middle") or (kind == "last" and step < HEADS - LEAD)

        def pv_now(kind, step):
            return {"first": step >= GROUP, "drain": step < GROUP}.get(kind, True)

        block = ctx.enter_context(nc.Block())

        @block.sync
        def _(sp):
            sp.wait_ge(consts, 1)
            for parity in range(2):
                sp.dma_start(stackK[KMAX:KALL, parity, :, :],
                             minus_one[:].unsqueeze(1).to_broadcast([2, HEADS, SEQ])).then_inc(ones_in, 16)
            prefetch(sp)

            def stack_rows(n, seq, parity):
                stack = stackQ if n == "q" else stackK
                for j, done in enumerate((part1_done[n], part2_done[n], part3_done[n])):
                    sp.wait_ge(done, seq + 1)
                    for other in range(3):
                        pair = 3 * j + other if n == "q" else 3 * other + j
                        sp.dma_start(stack[D * pair:D * (pair + 1), parity, :, :],
                                     part[n][j][:]).then_inc(rows_in[n], 16)

            def max_rows(group, parity, g):
                sp.wait_ge(maxT_done, group + 1)
                for r in range(2):
                    sp.dma_start(stackQ[KMAX + r:KMAX + r + 1, parity, GROUP * g:GROUP * (g + 1), :],
                                 maxT[:, g % 2, r, :]).then_inc(maxrows_in, 16)

            stack_rows("q", 0, 0)
            stack_rows("k", 0, 0)
            max_rows(0, 0, 0)

            def iteration(i, parity, kind):
                if kind == "drain":
                    return
                max_rows(i * GROUPS + 1, parity, 1)
                if kind != "last":
                    stack_rows("q", i + 1, 1 - parity)
                    stack_rows("k", i + 1, 1 - parity)
                max_rows(i * GROUPS + 2, parity, 2)
                max_rows(i * GROUPS + 3, parity, 3)
                if kind != "last":
                    max_rows(i * GROUPS + 4, 1 - parity, 0)

            over_sequences(sp, iteration)

        @block.gpsimd
        def _(pool):
            pool.memset(minus_one[:], -1.0).then_inc(consts, 1)
            norms.pool_part(pool, 0)
            pool.memset(v_one[:], 0.0).then_inc(v_zero, 1)
            pool.wait_ge(v_zero, 1)
            pool.memset(v_one[:, :, :, :, D:D + 1], 1.0).then_inc(v_zero, 1)

            def add_bias(seq):
                pool.wait_ge(xn_done, (seq + 1) * TILES)
                rows = x[:, bass.ds(seq * TILES, TILES), :]
                pool.tensor_tensor(rows, rows, bo[:].unsqueeze(1).to_broadcast([P, TILES, P]),
                                   ALU.add).then_inc(bias_added, 1)

            def split(n, seq):
                pool.wait_ge(full_done[n], seq + 1)
                pool.wait_ge(part1_done[n], seq + 1)
                pool.tensor_tensor(rest[n][:], full[n][:], part[n][0][:], ALU.subtract).then_inc(rest_done[n], 1)
                pool.wait_ge(part2_done[n], seq + 1)
                pool.tensor_tensor(part[n][2][:], rest[n][:], part[n][1][:], ALU.subtract)\
                    .then_inc(part3_done[n], 1)

            pool.wait_ge(weights_in, N_LOADS * 16)
            add_bias(0)
            split("q", 0)
            split("k", 0)
            norms.pool_part(pool, 1)

            def iteration(i, parity, kind):
                if kind in ("first", "middle"):
                    add_bias(i + 1)
                    split("q", i + 1)
                    split("k", i + 1)

            over_sequences(pool, iteration)

        @block.scalar
        def _(act):
            def project(n, seq, use):
                bias = bq if n == "q" else bk
                act.wait_ge(misc_full, use + 1)
                if not (isinstance(seq, int) and seq == 0):
                    act.wait_ge(rows_in[n], seq * 16 * PAIRS)
                    act.wait_ge(rest_done[n], seq)
                act.activation(full[n][:], ps_misc[:], ACT.Identity, bias=bias[:]).then_inc(full_done[n], 1)
                act.activation(part[n][0][:], ps_misc[:], ACT.Identity, bias=bias[:]).then_inc(part1_done[n], 1)
                act.wait_ge(part1_done[n], seq + 1)
                act.wait_ge(full_done[n], seq + 1)
                act.sem_inc(misc_free, 1)

            def second_part(n, seq):
                act.wait_ge(rest_done[n], seq + 1)
                act.activation(part[n][1][:], rest[n][:], ACT.Copy).then_inc(part2_done[n], 1)

            def copy_xnT(seq, use):
                act.wait_ge(misc_full, use + 1)
                act.activation(xnT[:], ps_misc[:], ACT.Copy).then_inc(misc_free, 1)

            if out_major:
                for n, tile in (("q", wq), ("k", wk), ("v", wv), ("o", wo)):
                    use = misc.at(f"w_{n}")
                    act.wait_ge(misc_full, use + 1)
                    if n == "o":
                        act.activation(tile[:], ps_misc[:, 0:P], ACT.Copy).then_inc(misc_free, 1)
                    else:
                        act.activation(tile[:].rearrange("p (d h) -> p d h", d=D),
                                       ps_misc[:, 0:P].rearrange("p (h d) -> p d h", d=D),
                                       ACT.Copy).then_inc(misc_free, 1)
            act.wait_ge(weights_in, N_LOADS * 16)
            copy_xnT(0, misc.at("xnT"))
            project("q", 0, misc.at("q"))
            second_part("q", 0)
            project("k", 0, misc.at("k"))
            second_part("k", 0)

            def exponentials(i, step, half, kind):
                if local:
                    if step % 2 or half:
                        return
                    unit = i * (HEADS // 2) + step // 2
                    out_ap = probs[:, step % SLOTS:step % SLOTS + 2, :].rearrange("p h t -> p (h t)")
                else:
                    unit = (i * HEADS + step) * 2 + half
                    out_ap = probs[:, step % SLOTS, half * 2 * SEQ:(half + 1) * 2 * SEQ]
                act.wait_ge(exp_full, unit + 1)
                if step % GROUP == 0 and not half and not (kind == "first" and step < SLOTS):
                    act.wait_ge(pv_step, i * HEADS + step - GROUP)
                bank = ps_exp[(step // 2) % 2 if local else half]
                act.activation(out_ap, bank[:], ACT.Exp, scale=D ** -0.5).then_inc(exp_done, 1)

            def iteration(i, parity, kind):
                for step in range(HEADS if kind != "drain" else 11):
                    for half in range(2):
                        if kind != "drain":
                            exponentials(i, step, half, kind)
                        name = tasks[kind].get((step, half))
                        if name == "xnT":
                            copy_xnT(i + 1, misc.at(name, i, kind))
                        elif name in ("q", "k"):
                            project(name, i + 1, misc.at(name, i, kind))
                        elif name == "outT":
                            act.wait_ge(misc_full, misc.at(name, i, kind) + 1)
                            if kind != "first":
                                act.activation(outT_all[:], ps_misc[:], ACT.Copy).then_inc(misc_free, 1)
                        if kind in ("first", "middle") and (step, half) == (4, 0):
                            second_part("q", i + 1)
                        if kind in ("first", "middle") and (step, half) == (5, 1):
                            second_part("k", i + 1)
                        if half and step % GROUP == GROUP - 1 and pv_now(kind, step):
                            read = tasks[kind].get((step - 2, 1))
                            if read:
                                act.wait_ge(misc_full, misc.at(read, i, kind) + 1)
                            act.wait_ge(pv_step, i * HEADS + step + 1 - GROUP)
                            act.activation(outT[:, (step // GROUP + 1) % 2, :], ps_pv[:], ACT.Copy)\
                                .then_inc(outT_done, 1)

            over_sequences(act, iteration)

        @block.vector
        def _(dve):
            norms.vector_part(dve, 0)

            def norm_apply(seq, tiles):
                dve.wait_ge(norms.rstd_done, 1 if isinstance(seq, int) and seq == 0 else 2)
                for t in tiles:
                    n = seq * TILES + t
                    dve.tensor_scalar(xn[:, t, :], x[:, n, :], norms.mean_var[:, n, 0:1],
                                      norms.rstd[:, bass.ds(n, 1)], ALU.subtract, ALU.mult).then_inc(xn_done, 1)

            def values(seq, parity, use):
                dve.wait_ge(misc_full, use + 1)
                dve.tensor_tensor(v_one[:, parity, :, :, 0:D],
                                  ps_misc[:].rearrange("p (t d h) -> p t h d", t=TILES, d=D),
                                  bv[:].rearrange("p (h d) -> p h d", d=D).unsqueeze(1)
                                  .to_broadcast([P, TILES, HEADS, D]),
                                  ALU.add).then_inc(v_done, 1)
                dve.wait_ge(v_done, seq + 1)
                dve.sem_inc(misc_free, 1)

            def max_parts(group, g, use):
                dve.wait_ge(misc_full, use + 1)
                if group is not None:
                    dve.wait_ge(maxrows_in, 32 * group)
                dve.tensor_copy(maxT[:, g % 2, 0, :], ps_misc[0:GROUP * TILES, 0:P]).then_inc(maxT1_done, 1)
                dve.wait_ge(maxT1_done, (0 if group is None else group + 1) + 1)
                dve.tensor_tensor(maxT[:, g % 2, 1, :], ps_misc[0:GROUP * TILES, 0:P],
                                  maxT[:, g % 2, 0, :], ALU.subtract).then_inc(maxT_done, 1)
                dve.wait_ge(maxT_done, (0 if group is None else group + 1) + 1)
                dve.sem_inc(misc_free, 1)

            def maxima(head, step, units):
                for u in units:
                    unit = head * MAX_UNITS + u
                    dve.wait_ge(max_full, unit + 1)
                    slot = (step // GROUP) % 2
                    col = (step % GROUP) * TILES
                    if local:
                        dve.tensor_reduce(rowmax[:, slot, col:col + TILES],
                                          ps_max[step % 2][:].rearrange("p (t k) -> p t k", t=TILES),
                                          AX.X, ALU.max).then_inc(max_done, 1)
                    else:
                        dve.tensor_reduce(rowmax[:, slot, col + u:col + u + 1], ps_max[u % 2][:],
                                          AX.X, ALU.max).then_inc(max_done, 1)

            dve.wait_ge(weights_in, N_LOADS * 16)
            if not out_major:
                for n, tile in (("q", wq), ("k", wk), ("v", wv)):
                    dve.tensor_copy(tile[:].rearrange("p (d h) -> p d h", d=D),
                                    raw[n][:].rearrange("p (h d) -> p d h", d=D)).then_inc(w_ready, 1)
                dve.tensor_copy(wo[:], raw["o"][:]).then_inc(w_ready, 1)
            norm_apply(0, range(TILES))
            if rest_of_x is not None:
                dve.wait_ge(rest_of_x, 16)
            norms.vector_part(dve, 1)
            dve.wait_ge(v_zero, 2)
            values(0, 0, misc.at("v"))
            for head in range(LEAD):
                maxima(head, head, range(MAX_UNITS))
            max_parts(None, 0, misc.at("max0"))

            def normalise(group, g, use):
                dve.wait_ge(misc_full, use + 1)
                block_ = ps_misc[:].rearrange("p (t j c) -> p t j c", t=TILES, j=GROUP)
                dve.reciprocal(rsum[:], block_[:, :, :, D]).then_inc(rsum_done, 1)
                dve.wait_ge(rsum_done, group + 1)
                heads = out[:].rearrange("p t (h d) -> p t h d", d=D)[:, :, GROUP * g:GROUP * (g + 1), :]
                dve.tensor_tensor(heads, block_[:, :, :, 0:D],
                                  rsum[:].unsqueeze(3).to_broadcast([P, TILES, GROUP, D]),
                                  ALU.mult).then_inc(out_done, 1)
                dve.wait_ge(out_done, group + 1)
                dve.sem_inc(misc_free, 1)

            def bank_task(i, parity, kind, step, name):
                use = misc.at(name, i, kind)
                if name[:3] == "max":
                    max_parts(i * GROUPS + (step // GROUP), int(name[3]), use)
                elif name in ("out0", "out1", "out2", "out3"):
                    normalise(i * GROUPS + step // GROUP - 2, int(name[3]), use)
                elif name == "v":
                    values(i + 1, 1 - parity, use)
                elif name == "y":
                    dve.wait_ge(misc_full, use + 1)
                    dve.wait_ge(bias_added, i)
                    rows = x[:, bass.ds((i - 1) * TILES, TILES), :]
                    dve.tensor_tensor(rows, rows, ps_misc[:].rearrange("p (t d) -> p t d", t=TILES),
                                      ALU.add).then_inc(misc_free, 1)

            def iteration(i, parity, kind):
                nxt = kind in ("first", "middle")
                steps = range(HEADS if kind != "drain" else 11)
                for step in steps:
                    for half in range(2):
                        if max_now(kind, step):
                            units = range(MAX_UNITS)[2 * half:2 * half + 2]
                            maxima(i * HEADS + step + LEAD, (step + LEAD) % HEADS, units)
                        if (step, half) in tasks[kind]:
                            bank_task(i, parity, kind, step, tasks[kind][step, half])
                        if nxt and step < 2:
                            norm_apply(i + 1, (2 * step + half,))

            over_sequences(dve, iteration)

        @block.tensor
        def _(pe):
            def free(use):
                if not (isinstance(use, int) and use == 0):
                    pe.wait_ge(misc_free, use)

            def transposed_norm(seq, use):
                pe.wait_ge(xn_done, (seq + 1) * TILES)
                free(use)
                for t in range(TILES):
                    last = pe.transpose(ps_misc[:, P * t:P * (t + 1)], xn[:, t, :], ident[:])
                last.then_inc(misc_full, 1)

            def projection(tile, use):
                free(use)
                pe.matmul(ps_misc[:], tile[:], xnT[:], start=True, stop=True).then_inc(misc_full, 1)

            def value_projection(use):
                free(use)
                for t in range(TILES):
                    last = pe.matmul(ps_misc[:, P * t:P * (t + 1)], xnT[:, P * t:P * (t + 1)], wv[:],
                                     start=True, stop=True)
                last.then_inc(misc_full, 1)

            def max_transpose(slot, maxima_done, use):
                pe.wait_ge(max_done, maxima_done)
                free(use)
                pe.transpose(ps_misc[0:GROUP * TILES, 0:P], rowmax[:, slot, :], ident[:]).then_inc(misc_full, 1)

            def scores_for_max(head, step, parity, units):
                for u in units:
                    unit = head * MAX_UNITS + u
                    if not (isinstance(unit, int) and unit < 2):
                        pe.wait_ge(max_done, unit - 1)
                    bank = ps_max[step % 2 if local else u % 2]
                    q, k = stackQ[0:KMAX, parity, step, :], stackK[0:KMAX, parity, step, :]
                    if local:
                        for t in range(TILES):
                            tile = slice(P * t, P * (t + 1))
                            last = pe.matmul(bank[:, tile], q[:, tile], k[:, tile], start=True, stop=True)
                    else:
                        last = pe.matmul(bank[:], q[:, P * u:P * (u + 1)], k, start=True, stop=True)
                    last.then_inc(max_full, 1)

            def scores_for_exp(i, step, half, parity, kind):
                if step % GROUP == 0 and not half:
                    pe.wait_ge(maxrows_in, 32 * (i * GROUPS + step // GROUP + 1))
                if local:
                    if step % 2 or half:
                        return
                    unit = i * (HEADS // 2) + step // 2
                    bank = ps_exp[(step // 2) % 2]
                else:
                    unit = (i * HEADS + step) * 2 + half
                    bank = ps_exp[half]
                if not (isinstance(unit, int) and unit < 2):
                    pe.wait_ge(exp_done, unit - 1)
                if local:
                    for h in range(2):
                        for t in range(TILES):
                            tile = slice(P * t, P * (t + 1))
                            last = pe.matmul(bank[:, h * SEQ + P * t:h * SEQ + P * (t + 1)],
                                             stackK[0:KALL, parity, step + h, tile],
                                             stackQ[0:KALL, parity, step + h, tile], start=True, stop=True)
                else:
                    for t in range(2):
                        kt = 2 * half + t
                        last = pe.matmul(bank[:, t * SEQ:(t + 1) * SEQ],
                                         stackK[0:KALL, parity, step, P * kt:P * (kt + 1)],
                                         stackQ[0:KALL, parity, step, :], start=True, stop=True)
                last.then_inc(exp_full, 1)

            def weigh_values(i, step, parity, kind):
                group_heads = (step - GROUP) % HEADS // GROUP * GROUP
                par = parity if step >= GROUP else 1 - parity
                kt = step % GROUP
                if kt == 0:
                    pe.wait_ge(v_done, i + 1 if step >= GROUP else i)
                    done = i * HEADS + step
                    pe.wait_ge(exp_done, i * (HEADS // 2) + step // 2 if local else 2 * done)
                    if not (kind == "first" and step == GROUP):
                        pe.wait_ge(outT_done, i * GROUPS + step // GROUP - 1)
                for j in range(GROUP):
                    head = group_heads + j
                    tile = slice(P * kt, P * (kt + 1))
                    lhs = v_one[:, par, kt, head, :]
                    if local:
                        last = pe.matmul(ps_pv[32 * j:32 * (j + 1), tile], lhs,
                                         probs[:, head % SLOTS, tile], start=True, stop=True)
                    else:
                        last = pe.matmul(ps_pv[32 * j:32 * (j + 1), :], lhs,
                                         probs[:, head % SLOTS, SEQ * kt:SEQ * (kt + 1)],
                                         start=(kt == 0), stop=(kt == TILES - 1))
                last.then_inc(pv_step, 1)

            def group_transpose(group, g, use):
                pe.wait_ge(outT_done, group + 1)
                free(use)
                for t in range(TILES):
                    last = pe.transpose(ps_misc[:, P * t:P * (t + 1)], outT[:, g % 2, P * t:P * (t + 1)], ident[:])
                last.then_inc(misc_full, 1)

            def all_heads_transpose(seq, use):
                pe.wait_ge(out_done, (seq + 1) * GROUPS)
                free(use)
                for t in range(TILES):
                    last = pe.transpose(ps_misc[:, P * t:P * (t + 1)], out[:, t, :], ident[:])
                last.then_inc(misc_full, 1)

            def output_projection(use):
                free(use)
                for t in range(TILES):
                    last = pe.matmul(ps_misc[:, P * t:P * (t + 1)], outT_all[:, P * t:P * (t + 1)], wo[:],
                                     start=True, stop=True)
                last.then_inc(misc_full, 1)

            pe.wait_ge(weights_in, N_LOADS * 16)
            if out_major:
                for n in "qkvo":
                    free(misc.at(f"w_{n}"))
                    pe.transpose(ps_misc[:, 0:P], raw[n][:], ident[:]).then_inc(misc_full, 1)
            else:
                pe.wait_ge(w_ready, 4)
            transposed_norm(0, misc.at("xnT"))
            projection(wq, misc.at("q"))
            projection(wk, misc.at("k"))
            value_projection(misc.at("v"))
            for n in "qk":
                pe.wait_ge(rows_in[n], 16 * PAIRS)
            for head in range(LEAD):
                scores_for_max(head, head, 0, range(MAX_UNITS))
            max_transpose(0, GROUP * MAX_UNITS, misc.at("max0"))
            pe.wait_ge(ones_in, 32)

            def iteration(i, parity, kind):
                for step in range(HEADS if kind != "drain" else 11):
                    ahead = step + LEAD
                    for half in range(2):
                        if max_now(kind, step):
                            par = parity if ahead < HEADS else 1 - parity
                            if ahead == HEADS and not half:
                                for n in "qk":
                                    pe.wait_ge(rows_in[n], (i + 2) * 16 * PAIRS)
                            units = range(MAX_UNITS)[2 * half:2 * half + 2]
                            scores_for_max(i * HEADS + ahead, ahead % HEADS, par, units[:1])
                        if kind != "drain":
                            scores_for_exp(i, step, half, parity, kind)
                        if max_now(kind, step):
                            scores_for_max(i * HEADS + ahead, ahead % HEADS, par, units[1:])
                        name = tasks[kind].get((step, half))
                        use = misc.at(name, i, kind) if name else None
                        if name == "xnT":
                            transposed_norm(i + 1, use)
                        elif name == "q":
                            projection(wq, use)
                        elif name == "k":
                            projection(wk, use)
                        elif name == "v":
                            value_projection(use)
                        elif name == "outT":
                            all_heads_transpose(i - 1, use)
                        elif name == "y":
                            output_projection(use)
                        elif name and name[:3] == "max":
                            g = int(name[3])
                            max_transpose(g % 2, (i * HEADS + step + 2 * GROUP) * MAX_UNITS, use)
                        elif name:
                            group_transpose(i * GROUPS + step // GROUP - 2, int(name[3]), use)
                        if half and pv_now(kind, step):
                            weigh_values(i, step, parity, kind)

            over_sequences(pe, iteration)


class Norms:

    def __init__(self, s, x):
        tiles = SEQS * TILES
        self.x = x
        self.stats = s.sb("stats", [P, tiles, 6])
        self.mean_var = s.sb("mean_var", [P, tiles, 2])
        self.var_eps = s.sb("var_eps", [P, tiles])
        self.power = s.sb("power", [P, tiles])
        self.rstd = s.sb("rstd", [P, tiles])
        self.stats_done = s.sem("stats_done")
        self.aggr_done = s.sem("aggr_done")
        self.eps_done = s.sem("eps_done")
        self.power_set = s.sem("power_set")
        self.rstd_done = s.sem("rstd_done")

    BATCHES = (slice(0, TILES), slice(TILES, SEQS * TILES))

    def vector_part(self, dve, batch):
        tiles = self.BATCHES[batch]
        for t in range(tiles.start, tiles.stop):
            dve.bn_stats(self.stats[:, t, :], self.x[:, t, :]).then_inc(self.stats_done, 1)
        dve.wait_ge(self.stats_done, tiles.stop)
        for t in range(tiles.start, tiles.stop):
            dve.bn_aggr(self.mean_var[:, t, :], self.stats[:, t, :]).then_inc(self.aggr_done, 1)
        dve.wait_ge(self.aggr_done, tiles.stop)
        dve.tensor_scalar(self.var_eps[:, tiles], self.mean_var[:, tiles, 1], EPS, None, ALU.add)\
            .then_inc(self.eps_done, 1)

    def pool_part(self, pool, batch):
        tiles = self.BATCHES[batch]
        if batch == 0:
            pool.memset(self.power[:], -0.5).then_inc(self.power_set, 1)
            pool.wait_ge(self.power_set, 1)
        pool.wait_ge(self.eps_done, batch + 1)
        pool.tensor_tensor(self.rstd[:, tiles], self.var_eps[:, tiles], self.power[:, tiles], ALU.pow)\
            .then_inc(self.rstd_done, 1)


class FfnWeights:

    CH = 4
    KEYS = 64
    LOADS = 1 + 2 * CH + 6 + 2

    def __init__(self, nc, ctx, name, w):
        def sb(tile, shape, ctx=ctx):
            return ctx.enter_context(nc.sbuf_tensor(f"{name}_{tile}", shape, F32))
        CH = self.CH
        self.w = w
        self.w_sim = sb("w_sim", [P, CH * P])
        self.downT, self.up = sb("downT", [P, CH, P]), sb("up", [P, CH, P])
        self.wg, self.wu, self.wd = (sb(n, [P, CH, P]) for n in ("wg", "wu", "wd"))
        self.bg, self.bu, self.half_bg = (sb(n, [P, CH]) for n in ("bg", "bu", "half_bg"))
        self.bd = sb("bd", [P, P])
        self.loaded = ctx.enter_context(nc.semaphore(f"{name}_loaded"))
        self.keys_zero = ctx.enter_context(nc.semaphore(f"{name}_keys_zero"))
        self.raw_ctx = ExitStack()
        self.wq, self.down = sb("wq", [P, CH, P], self.raw_ctx), sb("down", [P, CH, P], self.raw_ctx)
        self.keys = sb("keys", [P, CH, P], self.raw_ctx)

    def clear_keys(self, pool):
        pool.memset(self.keys[:], 0.0).then_inc(self.keys_zero, 1)

    def load(self, sp):
        w, CH, KEYS = self.w, self.CH, self.KEYS

        def load(dst, src, **kw):
            sp.dma_start(dst, src, **kw).then_inc(self.loaded, 16)

        load(self.wq[:].rearrange("p c n -> p (c n)"), w["Wq"])
        sp.wait_ge(self.keys_zero, 1)
        for c in range(CH):
            for hh in range(2):
                rows = slice(KEYS * hh, KEYS * (hh + 1))
                load(self.keys[rows, c, rows], w["keys"][2 * (c % 2) + hh, :, c // 2, :])
        load(self.down[:], w["down_embed"].rearrange("(c p) d -> p c d", p=P))
        load(self.wg[:].rearrange("p c n -> p (c n)"), w["Wg"])
        load(self.wu[:].rearrange("p c n -> p (c n)"), w["Wu"])
        load(self.wd[:], w["Wd"].rearrange("(c p) d -> p c d", p=P))
        load(self.up[:], w["up_embed"].rearrange("(c p) d -> p c d", p=P))
        load(self.bd[:], w["bd"].partition_broadcast(P))
        load(self.bg[:], w["bg"].rearrange("(c p) -> p c", p=P), allow_slow_non_contiguous=True)
        load(self.bu[:], w["bu"].rearrange("(c p) -> p c", p=P), allow_slow_non_contiguous=True)


def product_key_ffn(nc, stage, x, ident, banks, weights, prepare):
    PK_HEADS = 4
    KEYS = 64
    TOP = 8
    EXPERTS = 512
    ROWS = EXPERTS // KEYS
    CH = EXPERTS // P
    N_TILES = SEQS * TILES

    ctx = ExitStack()
    with ctx:
        s = Scope(nc, ctx, stage, banks)
        norms = Norms(s, x)
        w_sim, downT, up = weights.w_sim, weights.downT, weights.up
        wg, wu, wd, bg, bu, bd, half_bg = (weights.wg, weights.wu, weights.wd, weights.bg, weights.bu, weights.bd,
                                           weights.half_bg)
        if prepare:
            wq, keys, down = weights.wq, weights.keys, weights.down
            wqT = s.sb("wqT", [P, CH, P])
            keysT = s.sb("keysT", [P, CH, P])
        xn = s.sb("xn", [P, TILES, P])
        xnT = s.sb("xnT", [P, 2, SEQ])
        sim = s.sb("sim", [P, 2, 2, PK_HEADS, KEYS])
        top = s.sb("top", [P, 2, PK_HEADS, TOP])
        cand = s.sb("cand", [P, PK_HEADS, TOP, TOP])
        best = s.sb("best", [P, 2, PK_HEADS, TOP])
        neg_best = s.sb("neg_best", [P, 2, PK_HEADS])
        best_less = s.sb("best_less", [P, 2, PK_HEADS, TOP])
        best_exp = s.sb("best_exp", [P, 2, PK_HEADS, TOP])
        zsum = s.sb("zsum", [P, PK_HEADS])
        zinv = s.sb("zinv", [P, 2, PK_HEADS])
        pair = s.sb("pair", [P, 2, PK_HEADS, ROWS, KEYS])
        pair_exp = s.sb("pair_exp", [P, 2, PK_HEADS, EXPERTS])
        gate = s.sb("gate", [P, 2, PK_HEADS, EXPERTS])
        gsum = s.sb("gsum", [P, PK_HEADS])
        left = s.sb("left", [P, PK_HEADS])
        diag = s.sb("diag", [P, 2, PK_HEADS, P])
        th = s.sb("th", [P, 2, SEQ])
        sg = s.sb("sg", [P, 2, SEQ])
        mlp_silu = s.sb("mlp_silu", [P, SEQ])
        mlp_hidden = s.sb("mlp_hidden", [P, 2, CH, SEQ])
        expert_silu = s.sb("expert_silu", [P, 2, CH, SEQ])
        expert_hidden = s.sb("expert_hidden", [P, 2, CH, P])

        ps_sim = s.ps()
        ps_gate = [s.ps() for j in range(2)]
        ps_out = s.ps()
        ps_xnT = s.ps()
        ps_wg, ps_wu, ps_we = s.ps(), s.ps(), s.ps()

        prep_full = s.sem("prep_full")
        prep_free = s.sem("prep_free")
        half_done = s.sem("half_done")
        xn_done = s.sem("xn_done")
        bias_added = s.sem("bias_added")
        xnT_full = s.sem("xnT_full")
        xnT_done = s.sem("xnT_done")
        sim_full = s.sem("sim_full")
        sim_done = s.sem("sim_done")
        top_done = s.sem("top_done")
        cand_done = s.sem("cand_done")
        best_done = s.sem("best_done")
        passed_dve = s.sem("passed_dve")
        passed_pool = s.sem("passed_pool")
        less_done = s.sem("less_done")
        bexp_done = s.sem("bexp_done")
        zsum_done = s.sem("zsum_done")
        zinv_done = s.sem("zinv_done")
        pair_done = s.sem("pair_done")
        pexp_done = s.sem("pexp_done")
        masked_done = s.sem("masked_done")
        left_done = s.sem("left_done")
        gate_done = s.sem("gate_done")
        diag_done = s.sem("diag_done")
        gateT_full = s.sem("gateT_full")
        eh_done = s.sem("eh_done")
        out_full = s.sem("out_full")
        out_done = s.sem("out_done")
        chunk_full = s.sem("chunk_full")
        th_done = s.sem("th_done")
        sg_done = s.sem("sg_done")
        ms_done = s.sem("ms_done")
        mh_done = s.sem("mh_done")
        es_done = s.sem("es_done")
        weights_in, n_loads = weights.loaded, weights.LOADS
        block = ctx.enter_context(nc.Block())

        @block.gpsimd
        def _(pool):
            norms.pool_part(pool, 0)
            norms.pool_part(pool, 1)
            pool.wait_ge(weights_in, n_loads * 16)

            def add_bias(seq):
                pool.wait_ge(xn_done, (seq + 1) * TILES)
                rows = x[:, bass.ds(seq * TILES, TILES), :]
                pool.tensor_tensor(rows, rows, bd[:].unsqueeze(1).to_broadcast([P, TILES, P]),
                                   ALU.add).then_inc(bias_added, 1)

            def pair_sums(n, b):
                pool.wait_ge(sim_done, n + 1)
                if not (isinstance(n, int) and n < 2):
                    pool.wait_ge(pexp_done, (n - 1) * PK_HEADS)
                pool.tensor_tensor(pair[:, b], sim[:, b, 0, :, 0:ROWS].unsqueeze(3)
                                   .to_broadcast([P, PK_HEADS, ROWS, KEYS]),
                                   sim[:, b, 1].unsqueeze(2).to_broadcast([P, PK_HEADS, ROWS, KEYS]),
                                   ALU.add).then_inc(pair_done, 1)

            def diagonals(n, b):
                pool.wait_ge(zinv_done, n + 1)
                if not (isinstance(n, int) and n < 2):
                    pool.wait_ge(gateT_full, n - 1)
                    pool.sem_inc(passed_pool, 1)
                for h in range(PK_HEADS):
                    pool.tensor_scalar(diag[:, b, h, :], ident[:], zinv[:, b, h:h + 1], None,
                                       ALU.mult).then_inc(diag_done, 1)

            add_bias(0)
            pair_sums(0, 0)
            pair_sums(1, 1)
            diagonals(0, 0)

            def iteration(i, parity, kind):
                if kind in ("first", "middle"):
                    add_bias(i + 1)
                if kind == "drain":
                    return
                for t in range(TILES):
                    if kind != "last" or t + 1 < TILES:
                        diagonals(i * TILES + t + 1, (t + 1) % 2)
                    if kind != "last" or t + 2 < TILES:
                        pair_sums(i * TILES + t + 2, t % 2)

            over_sequences(pool, iteration)

        @block.scalar
        def _(act):
            if prepare:
                for use, (dst, j) in enumerate([(t_, c) for c in range(CH) for t_ in (wqT, keysT, downT)]):
                    act.wait_ge(prep_full, use + 1)
                    act.activation(dst[:, j, :], (ps_wg, ps_wu)[use % 2][:, 0:P], ACT.Copy).then_inc(prep_free, 1)
                act.wait_ge(prep_full, 3 * CH + 1)
                act.activation(w_sim[:], ps_sim[:], ACT.Copy).then_inc(prep_free, 1)

            def copy_xnT(seq, b):
                act.wait_ge(xnT_full, seq + 1)
                act.activation(xnT[:, b, :], ps_xnT[:], ACT.Copy).then_inc(xnT_done, 1)

            def copy_sim(n, b):
                act.wait_ge(sim_full, n + 1)
                if not (isinstance(n, int) and n < 2):
                    act.wait_ge(pair_done, n - 1)
                    act.wait_ge(top_done, (n - 1) * 2 * PK_HEADS)
                act.activation(sim[:, b], ps_sim[:], ACT.Copy).then_inc(sim_done, 1)

            def exponentials(n, b):
                act.wait_ge(less_done, n + 1)
                if not (isinstance(n, int) and n < 2):
                    act.wait_ge(zsum_done, n - 1)
                act.activation(best_exp[:, b], best_less[:, b], ACT.Exp).then_inc(bexp_done, 1)
                act.wait_ge(pair_done, n + 1)
                if not (isinstance(n, int) and n < 2):
                    act.wait_ge(masked_done, (n - 1) * PK_HEADS)
                for h in range(PK_HEADS):
                    act.activation(pair_exp[:, b, h, :], pair[:, b, h].rearrange("p a k -> p (a k)"), ACT.Exp,
                                   bias=neg_best[:, b, h:h + 1]).then_inc(pexp_done, 1)

            def chunk_sigmoids(m, c):
                act.wait_ge(chunk_full, 3 * m + 3)
                if not (isinstance(m, int) and m == 0):
                    act.wait_ge(es_done, m)
                act.activation(th[:, 0, :], ps_wg[:], ACT.Tanh, bias=half_bg[:, c:c + 1], scale=0.5)\
                    .then_inc(th_done, 1)
                act.activation(th[:, 1, :], ps_we[:], ACT.Tanh, scale=0.5).then_inc(th_done, 1)
                act.wait_ge(th_done, 2 * m + 2)
                act.activation(sg[:], th[:], ACT.Copy, bias=0.5, scale=0.5).then_inc(sg_done, 1)

            copy_xnT(0, 0)
            copy_sim(0, 0)
            copy_sim(1, 1)
            if prepare:
                act.wait_ge(half_done, 1)
            for c in range(CH):
                chunk_sigmoids(c, c)
            exponentials(0, 0)
            exponentials(1, 1)

            def iteration(i, parity, kind):
                if kind == "drain":
                    return
                for t in range(TILES):
                    if kind != "last" or t + 2 < TILES:
                        copy_sim(i * TILES + t + 2, t % 2)
                    if kind != "last" and t == 0:
                        copy_xnT(i + 1, 1 - parity)
                    if kind != "last":
                        chunk_sigmoids((i + 1) * CH + t, t)
                    if kind != "last" or t + 2 < TILES:
                        exponentials(i * TILES + t + 2, t % 2)

            over_sequences(act, iteration)

        @block.vector
        def _(dve):
            norms.vector_part(dve, 0)
            dve.wait_ge(weights_in, n_loads * 16)
            if prepare:
                dve.tensor_scalar(half_bg[:], bg[:], 0.5, None, ALU.mult).then_inc(half_done, 1)

            def norm_apply(seq):
                dve.wait_ge(norms.rstd_done, 1 if isinstance(seq, int) and seq == 0 else 2)
                if not (isinstance(seq, int) and seq == 0):
                    dve.wait_ge(xnT_full, seq)
                for t in range(TILES):
                    n = seq * TILES + t
                    dve.tensor_scalar(xn[:, t, :], x[:, n, :], norms.mean_var[:, n, 0:1],
                                      norms.rstd[:, bass.ds(n, 1)], ALU.subtract, ALU.mult).then_inc(xn_done, 1)

            def top_pairs(n, b):
                dve.wait_ge(sim_done, n + 1)
                dve.sem_inc(passed_dve, 1)
                for side in range(2):
                    for h in range(PK_HEADS):
                        dve.max(top[:, side, h, :], sim[:, b, side, h, :]).then_inc(top_done, 1)
                dve.wait_ge(top_done, (n + 1) * 2 * PK_HEADS)
                dve.tensor_tensor(cand[:], top[:, 0].unsqueeze(3).to_broadcast([P, PK_HEADS, TOP, TOP]),
                                  top[:, 1].unsqueeze(2).to_broadcast([P, PK_HEADS, TOP, TOP]),
                                  ALU.add).then_inc(cand_done, 1)
                dve.wait_ge(cand_done, n + 1)
                if not (isinstance(n, int) and n < 2):
                    dve.wait_ge(pexp_done, (n - 1) * PK_HEADS)
                    dve.sem_inc(passed_dve, 1)
                for h in range(PK_HEADS):
                    dve.max(best[:, b, h, :], cand[:, h].rearrange("p a k -> p (a k)")).then_inc(best_done, 1)
                dve.wait_ge(best_done, (n + 1) * PK_HEADS)
                dve.tensor_scalar(neg_best[:, b], best[:, b, :, 0], -1.0, None, ALU.mult)
                dve.tensor_tensor(best_less[:, b], best[:, b],
                                  best[:, b, :, 0:1].to_broadcast([P, PK_HEADS, TOP]),
                                  ALU.subtract).then_inc(less_done, 1)

            def gates(n, b):
                dve.wait_ge(bexp_done, n + 1)
                dve.tensor_reduce(zsum[:], best_exp[:, b], AX.X, ALU.add).then_inc(zsum_done, 1)
                dve.wait_ge(zsum_done, n + 1)
                dve.reciprocal(zinv[:, b], zsum[:]).then_inc(zinv_done, 1)
                dve.wait_ge(pexp_done, (n + 1) * PK_HEADS)
                if not (isinstance(n, int) and n < 2):
                    dve.wait_ge(gateT_full, n - 1)
                for h in range(PK_HEADS):
                    dve.scalar_tensor_tensor(gate[:, b, h, :], pair[:, b, h].rearrange("p a k -> p (a k)"),
                                             best[:, b, h, TOP - 1:TOP], pair_exp[:, b, h, :],
                                             ALU.is_ge, ALU.mult, accum_out=gsum[:, h:h + 1])\
                        .then_inc(masked_done, 1)
                dve.wait_ge(masked_done, (n + 1) * PK_HEADS)
                dve.tensor_tensor(left[:], zsum[:], gsum[:], ALU.subtract).then_inc(left_done, 1)
                dve.wait_ge(left_done, n + 1)
                last = gate[:, b, :, EXPERTS - 1]
                dve.tensor_tensor(last, last, left[:], ALU.add).then_inc(gate_done, 1)

            def expert_products(n, b, seq_parity, t):
                dve.wait_ge(gateT_full, n + 1)
                if not (isinstance(n, int) and n < 2):
                    dve.wait_ge(out_full, n - 1)
                dve.tensor_tensor(expert_hidden[:, b], ps_gate[b][:].rearrange("p (c t) -> p c t", c=CH),
                                  expert_silu[:, seq_parity, :, P * t:P * (t + 1)],
                                  ALU.mult).then_inc(eh_done, 1)

            def add_out(n, seq):
                dve.wait_ge(out_full, n + 1)
                dve.wait_ge(bias_added, seq + 1)
                dve.tensor_tensor(x[:, n, :], x[:, n, :], ps_out[:, 0:P], ALU.add).then_inc(out_done, 1)

            def chunk_hidden(m, c, b):
                dve.wait_ge(sg_done, m + 1)
                dve.scalar_tensor_tensor(mlp_silu[:], ps_wg[:], bg[:, c:c + 1], sg[:, 0, :],
                                         ALU.add, ALU.mult).then_inc(ms_done, 1)
                dve.tensor_tensor(expert_silu[:, b, c, :], ps_we[:], sg[:, 1, :], ALU.mult).then_inc(es_done, 1)
                dve.wait_ge(ms_done, m + 1)
                dve.scalar_tensor_tensor(mlp_hidden[:, b, c, :], ps_wu[:], bu[:, c:c + 1], mlp_silu[:],
                                         ALU.add, ALU.mult).then_inc(mh_done, 1)

            norm_apply(0)
            norms.vector_part(dve, 1)
            top_pairs(0, 0)
            top_pairs(1, 1)
            for c in range(CH):
                chunk_hidden(c, c, 0)
            gates(0, 0)

            def iteration(i, parity, kind):
                if kind == "drain":
                    add_out(i * TILES - 1, i - 1)
                    return
                for t in range(TILES):
                    n = i * TILES + t
                    if kind != "last" and t == 0:
                        norm_apply(i + 1)
                    if kind != "last" or t + 1 < TILES:
                        gates(n + 1, (t + 1) % 2)
                    if kind != "last" or t + 2 < TILES:
                        top_pairs(n + 2, t % 2)
                    expert_products(n, t % 2, parity, t)
                    if not (kind == "first" and t == 0):
                        add_out(n - 1, i if t else i - 1)
                    if kind != "last":
                        chunk_hidden((i + 1) * CH + t, t, 1 - parity)

            over_sequences(dve, iteration)

        @block.tensor
        def _(pe):
            pe.wait_ge(weights_in, n_loads * 16)
            if prepare:
                for use, (src, j) in enumerate([(t_, c) for c in range(CH) for t_ in (wq, keys, down)]):
                    if use >= 2:
                        pe.wait_ge(prep_free, use - 1)
                    pe.transpose((ps_wg, ps_wu)[use % 2][:, 0:P], src[:, j, :], ident[:]).then_inc(prep_full, 1)
                pe.wait_ge(prep_free, 3 * CH)
                for c in range(CH):
                    last = pe.matmul(ps_sim[:, P * c:P * (c + 1)], wqT[:, c, :], keysT[:, c, :], start=True, stop=True)
                last.then_inc(prep_full, 1)

            def transposed_norm(seq):
                pe.wait_ge(xn_done, (seq + 1) * TILES)
                if not (isinstance(seq, int) and seq == 0):
                    pe.wait_ge(xnT_done, seq)
                for t in range(TILES):
                    last = pe.transpose(ps_xnT[:, P * t:P * (t + 1)], xn[:, t, :], ident[:])
                last.then_inc(xnT_full, 1)

            def similarities(n, seq, b, t):
                pe.wait_ge(xnT_done, seq + 1)
                if isinstance(n, int) and n == 0:
                    if prepare:
                        pe.wait_ge(prep_free, 3 * CH + 1)
                else:
                    pe.wait_ge(sim_done, n)
                pe.matmul(ps_sim[:], xnT[:, b, P * t:P * (t + 1)], w_sim[:], start=True, stop=True)\
                    .then_inc(sim_full, 1)

            def chunk(m, c, b):
                pe.wait_ge(xnT_done, m + 1 if isinstance(m, int) and m == 0 else 1)
                for k, (bank, tile) in enumerate(((ps_wg, wg), (ps_we, downT), (ps_wu, wu))):
                    if not (isinstance(m, int) and m == 0):
                        pe.wait_ge((ms_done, es_done, mh_done)[k], m)
                    pe.matmul(bank[:], tile[:, c, :], xnT[:, b, :], start=True, stop=True).then_inc(chunk_full, 1)

            def gate_transpose(n, b):
                pe.wait_ge(gate_done, n + 1)
                pe.wait_ge(diag_done, (n + 1) * PK_HEADS)
                if not (isinstance(n, int) and n < 2):
                    pe.wait_ge(eh_done, n - 1)
                for c in range(CH):
                    for h in range(PK_HEADS):
                        last = pe.matmul(ps_gate[b][:, P * c:P * (c + 1)], gate[:, b, h, P * c:P * (c + 1)],
                                         diag[:, b, h, :], start=(h == 0), stop=(h == PK_HEADS - 1))
                last.then_inc(gateT_full, 1)

            def output(n, b, seq_parity, t):
                pe.wait_ge(eh_done, n + 1)
                if not (isinstance(n, int) and n == 0):
                    pe.wait_ge(out_done, n)
                for c in range(CH):
                    pe.matmul(ps_out[:, 0:P], mlp_hidden[:, seq_parity, c, P * t:P * (t + 1)], wd[:, c, :],
                              start=(c == 0), stop=False)
                for c in range(CH):
                    last = pe.matmul(ps_out[:, 0:P], expert_hidden[:, b, c, :], up[:, c, :],
                                     start=False, stop=(c == CH - 1))
                last.then_inc(out_full, 1)

            transposed_norm(0)
            similarities(0, 0, 0, 0)
            similarities(1, 0, 0, 1)
            for c in range(CH):
                chunk(c, c, 0)

            def iteration(i, parity, kind):
                if kind == "drain":
                    pe.wait_ge(mh_done, i * CH)
                    output(i * TILES - 1, 1, 1 - parity, TILES - 1)
                    return
                for t in range(TILES):
                    n = i * TILES + t
                    if kind != "last" or t + 2 < TILES:
                        ahead = t + 2
                        if ahead < TILES:
                            similarities(n + 2, i, parity, ahead)
                        else:
                            similarities(n + 2, i + 1, 1 - parity, ahead - TILES)
                    gate_transpose(n, t % 2)
                    if t == 1:
                        pe.wait_ge(mh_done, (i + 1) * CH)
                    if not (kind == "first" and t == 0):
                        output(n - 1, (t - 1) % 2, parity if t else 1 - parity, (t - 1) % TILES)
                    if kind != "last" and t == 0:
                        transposed_norm(i + 1)
                    if kind != "last":
                        if t == 0:
                            pe.wait_ge(xnT_done, i + 2)
                        chunk((i + 1) * CH + t, t, 1 - parity)

            over_sequences(pe, iteration)


def linear_ffn(nc, stage, x, ident, banks, w, folded, folded_bias, fold, out_dram=None):
    CH = 4
    ctx = ExitStack()
    with ctx:
        s = Scope(nc, ctx, stage, banks)
        norms = Norms(s, x)
        w1 = s.sb("w1", [P, 2, CH, P])
        w2 = s.sb("w2", [P, 2, CH * P])
        w2T = s.sb("w2T", [P, CH, P])
        b1_rows = s.sb("b1_rows", [SEQS * CH, P])
        b1_cols = s.sb("b1_cols", [P, SEQS * CH])
        b2 = s.sb("b2", [P, SEQS, P])
        xn = s.sb("xn", [P, TILES, P])
        xnT = s.sb("xnT", [P, SEQ])
        ps_b1 = s.ps()
        ps_w2T = s.ps()
        ps_fold = s.ps()
        ps_bias = s.ps()
        ps_xnT = s.ps()
        ps_out = s.ps()

        bias_in = s.sem("bias_in")
        weights_in = [s.sem(f"weights_in{b}") for b in range(2)]
        b1_full = s.sem("b1_full")
        b1_done = s.sem("b1_done")
        w2T_full = s.sem("w2T_full")
        w2T_done = s.sem("w2T_done")
        fold_full = s.sem("fold_full")
        fold_done = s.sem("fold_done")
        fbias_done = s.sem("fbias_done")
        xn_done = s.sem("xn_done")
        bias_added = s.sem("bias_added")
        xnT_full = s.sem("xnT_full")
        xnT_done = s.sem("xnT_done")
        out_full = s.sem("out_full")
        out_done = s.sem("out_done")

        block = ctx.enter_context(nc.Block())

        if fold:
            @block.sync
            def _(sp):
                sp.dma_start(b1_rows[:], w["b1"].rearrange("g (c o) -> (g c) o", o=P)).then_inc(bias_in, 16)
                sp.dma_start(b2[:], w["b2"].partition_broadcast(P)).then_inc(bias_in, 16)

                def load(g, b):
                    sp.dma_start(w1[:, b], w["W1"][g].rearrange("(c o) h -> o c h", o=P)).then_inc(weights_in[b], 16)
                    sp.dma_start(w2[:, b], w["W2"][g]).then_inc(weights_in[b], 16)

                load(0, 0)
                load(1, 1)
                with sp.Fori(0, (SEQS - 2) // 2) as turn:
                    for b in range(2):
                        sp.wait_ge(fold_full, turn * 2 + b + 1)
                        load(turn * 2 + b + 2, b)

        if out_dram is not None:
            stored = s.sem("stored")

            @block.sync
            def _(sp):
                PARTS = 4
                for n in range(PARTS):
                    sp.wait_ge(out_done, (n + 1) * SEQS // PARTS)
                    tiles = slice(n * SEQS * TILES // PARTS, (n + 1) * SEQS * TILES // PARTS)
                    sp.dma_start(out_dram[:, tiles, :], x[:, tiles, :]).then_inc(stored, 16)
                sp.wait_ge(stored, PARTS * 16)

        @block.gpsimd
        def _(pool):
            norms.pool_part(pool, 0)
            norms.pool_part(pool, 1)
            with pool.Fori(0, SEQS) as i:
                pool.wait_ge(xn_done, (i + 1) * TILES)
                if fold:
                    pool.wait_ge(fbias_done, i + 1)
                rows = x[:, bass.ds(i * TILES, TILES), :]
                pool.tensor_tensor(rows, rows, folded_bias[:, bass.ds(i, 1), :].to_broadcast([P, TILES, P]),
                                   ALU.add).then_inc(bias_added, 1)

        @block.scalar
        def _(act):
            if fold:
                act.wait_ge(b1_full, 1)
                act.activation(b1_cols[:], ps_b1[:, 0:SEQS * CH], ACT.Copy).then_inc(b1_done, 1)

            def body(i, first):
                if fold:
                    act.wait_ge(w2T_full, i + 1)
                    if not first:
                        act.wait_ge(fold_full, i)
                    act.activation(w2T[:], ps_w2T[:], ACT.Copy).then_inc(w2T_done, 1)
                act.wait_ge(xnT_full, i + 1)
                if not first:
                    act.wait_ge(out_full, i)
                act.activation(xnT[:], ps_xnT[:], ACT.Copy).then_inc(xnT_done, 1)
                if fold:
                    act.wait_ge(fold_full, i + 1)
                    act.activation(folded[:, bass.ds(i, 1), :], ps_fold[:, 0:P], ACT.Copy).then_inc(fold_done, 1)

            body(0, True)
            with act.Fori(1, SEQS) as i:
                body(i, False)

        @block.vector
        def _(dve):
            norms.vector_part(dve, 0)
            if fold:
                dve.wait_ge(bias_in, 32)

            def apply(i, first):
                if not first:
                    dve.wait_ge(xnT_full, i)
                dve.wait_ge(norms.rstd_done, 1 if first else 2)
                for t in range(TILES):
                    n = i * TILES + t
                    dve.tensor_scalar(xn[:, t, :], x[:, n, :], norms.mean_var[:, n, 0:1],
                                      norms.rstd[:, bass.ds(n, 1)], ALU.subtract, ALU.mult).then_inc(xn_done, 1)
                if fold:
                    dve.wait_ge(fold_full, i + 1)
                    dve.tensor_tensor(folded_bias[:, bass.ds(i, 1), :], ps_bias[:, 0:P], b2[:, bass.ds(i, 1), :],
                                      ALU.add).then_inc(fbias_done, 1)

            def add_out(i):
                dve.wait_ge(out_full, i + 1)
                dve.wait_ge(bias_added, i + 1)
                rows = x[:, bass.ds(i * TILES, TILES), :]
                dve.tensor_tensor(rows, rows, ps_out[:].rearrange("p (t d) -> p t d", t=TILES),
                                  ALU.add).then_inc(out_done, 1)

            apply(0, True)
            norms.vector_part(dve, 1)
            with dve.Fori(1, SEQS) as i:
                apply(i, False)
                add_out(i - 1)
            add_out(SEQS - 1)

        @block.tensor
        def _(pe):
            if fold:
                pe.wait_ge(bias_in, 32)
                pe.transpose(ps_b1[:, 0:SEQS * CH], b1_rows[:], ident[0:SEQS * CH, 0:SEQS * CH]).then_inc(b1_full, 1)
                pe.wait_ge(b1_done, 1)

            def fold_group(i, b, turn, first):
                pe.wait_ge(weights_in[b], (turn + 1) * 32)
                if not first:
                    pe.wait_ge(w2T_done, i)
                for c in range(CH):
                    last = pe.transpose(ps_w2T[:, P * c:P * (c + 1)], w2[:, b, P * c:P * (c + 1)], ident[:])
                last.then_inc(w2T_full, 1)
                pe.wait_ge(w2T_done, i + 1)
                if not first:
                    pe.wait_ge(fold_done, i)
                    pe.wait_ge(fbias_done, i)
                for c in range(CH):
                    pe.matmul(ps_bias[:, 0:P], b1_cols_of(i, c), w2T[:, c, :], start=(c == 0), stop=(c == CH - 1))
                for c in range(CH):
                    last = pe.matmul(ps_fold[:, 0:P], w1[:, b, c, :], w2T[:, c, :], start=(c == 0), stop=(c == CH - 1))
                last.then_inc(fold_full, 1)

            def b1_cols_of(i, c):
                return b1_cols[:, i * CH + c:i * CH + c + 1].to_broadcast([P, P])

            def transposed_norm(i, first):
                pe.wait_ge(xn_done, (i + 1) * TILES)
                if not first:
                    pe.wait_ge(xnT_done, i)
                for t in range(TILES):
                    last = pe.transpose(ps_xnT[:, P * t:P * (t + 1)], xn[:, t, :], ident[:])
                last.then_inc(xnT_full, 1)

            def output(i, first):
                pe.wait_ge(xnT_done, i + 1)
                if fold:
                    pe.wait_ge(fold_done, i + 1)
                if not first:
                    pe.wait_ge(out_done, i)
                for t in range(TILES):
                    last = pe.matmul(ps_out[:, P * t:P * (t + 1)], xnT[:, P * t:P * (t + 1)],
                                     folded[:, bass.ds(i, 1), :], start=True, stop=True)
                last.then_inc(out_full, 1)

            for i in range(SEQS):
                if fold:
                    fold_group(i, i % 2, i // 2, i == 0)
                transposed_norm(i, i == 0)
                output(i, i == 0)


def wide_attention(nc, stage, x, ident, banks, w):
    D = 64
    PAIRS = HEADS // 2
    PROJ_LEAD = 3
    MAX_LEAD = 2
    SLOTS = 4
    SCALE = 1.0 / (D * D * HEADS)

    ctx = ExitStack()
    with ctx:
        s = Scope(nc, ctx, stage, banks)
        norms = Norms(s, x)
        w_part = {n: s.sb(f"w{n}", [P, 2, HEADS, D], F32R) for n in "qk"}
        wv = s.sb("wv", [P, HEADS, D])
        wo = s.sb("wo", [P, PAIRS, P])
        ones = s.sb("ones", [P, D])
        xn = s.sb("xn", [P, TILES, P])
        xnT = s.sb("xnT", [P, SEQ])
        xnT_part = s.sb("xnT_part", [P, 2, SEQ], F32R)
        q_ab = s.sb("q_ab", [P, SLOTS, 2, SEQ], F32R)
        q_am = s.sb("q_am", [D + 1, SLOTS, 2, SEQ], F32R)
        k_aa = s.sb("k_aa", [P, SLOTS, 2, SEQ], F32R)
        k_b1 = s.sb("k_b1", [D + 1, SLOTS, 2, SEQ], F32R)
        v = s.sb("v", [P, TILES, HEADS * D])
        rowmax = s.sb("rowmax", [P, 2, 2 * TILES])
        maxT = s.sb("maxT", [2 * TILES, 2, P], F32R)
        probs = s.sb("probs", [P, 2, 2, TILES * SEQ])
        part_sums = s.sb("part_sums", [P, 2, 2, SEQ])
        outT = s.sb("outT", [P, SEQ])
        sumT = s.sb("sumT", [P, SEQ])
        rsum = s.sb("rsum", [P, TILES, 2])
        normed = s.sb("normed", [P, PAIRS, SEQ])

        ps_proj = s.ps()
        ps_max = [s.ps() for j in range(2)]
        ps_exp = [s.ps() for j in range(3)]
        ps_pv = s.ps()
        ps_misc = s.ps()

        weights_in = s.sem("weights_in")
        consts = s.sem("consts")
        xn_done = s.sem("xn_done")
        proj_full = s.sem("proj_full")
        proj_free = s.sem("proj_free")
        w_first_done = s.sem("w_first_done")
        w_parts_done = s.sem("w_parts_done")
        xa_done = s.sem("xa_done")
        qa_done = s.sem("qa_done")
        copied = s.sem("copied")
        ka_done = s.sem("ka_done")
        max_full = s.sem("max_full")
        max_done = s.sem("max_done")
        maxT_done = s.sem("maxT_done")
        maxrow_in = [s.sem(f"maxrow_in{b}") for b in range(2)]
        exp_full = s.sem("exp_full")
        exp_done = s.sem("exp_done")
        half_done = s.sem("half_done")
        part_done = s.sem("part_done")
        pv_full = s.sem("pv_full")
        outT_done = s.sem("outT_done")
        misc_full = s.sem("misc_full")
        misc_free = s.sem("misc_free")
        rsum_done = s.sem("rsum_done")
        normed_done = s.sem("normed_done")

        def projects(kind, step):
            return kind in ("first", "middle") or (kind == "last" and step < PAIRS - PROJ_LEAD)

        def maximises(kind, step):
            return kind in ("first", "middle") or (kind == "last" and step < PAIRS - MAX_LEAD)

        def moves_maxima(kind, step):
            return kind in ("first", "middle") or (kind == "last" and step < PAIRS - 1)

        def weighs(kind, step):
            return {"first": step >= 1, "drain": step < 1}.get(kind, True)

        def normalises(kind, step):
            return {"first": step >= 2, "drain": step < 2}.get(kind, True)

        def moves(i, step):
            return i * (PAIRS // 2) + step // 2 + 1

        def proj_at(step):
            return {1: "q", 2: "k"} if step == 5 else {0: "q", 2: "k"}

        def v_uses(kind, step, u):
            ahead = {(5, 3): (0,), (6, 1): (2,), (6, 3): (4,), (7, 1): (6,)}
            now = {(1, 1): (1,), (2, 1): (3,), (3, 1): (5,), (4, 1): (7,)}
            return (ahead.get((step, u), ()) if kind in ("first", "middle") else ()) \
                + (now.get((step, u), ()) if kind != "drain" else ())

        def proj_uses(kind):
            names = []
            for step in range(PAIRS if kind != "drain" else 0):
                nxt = kind in ("first", "middle")
                if nxt and step == 5:
                    names.append((step, "xnT"))
                for u in range(4):
                    if projects(kind, step) and u in proj_at(step):
                        names.append((step, proj_at(step)[u]))
                    names += [(step, f"v{c}") for c in v_uses(kind, step, u)]
            return names

        def misc_uses(kind):
            names = []
            for step in range(PAIRS if kind != "drain" else 2):
                for n in ("sum", "max", "sumT", "recip"):
                    if moves_maxima(kind, step) if n == "max" else normalises(kind, step):
                        names.append((step, n))
                if step == 1 and kind != "first":
                    names.append("y")
            return names

        proj = Uses(["xnT"] + [f"v{c}" for c in range(0, 2 * TILES, 2)]
                    + [(p, n) for p in range(PROJ_LEAD) for n in "qk"], proj_uses)
        misc = Uses(["max"], misc_uses)

        n_loads = 5
        w_whole = [probs[:, 0, n, 0:HEADS * D].rearrange("p (h d) -> p h d", h=HEADS) for n in range(2)]

        block = ctx.enter_context(nc.Block())

        @block.sync
        def _(sp):
            for n in range(2):
                sp.dma_start(w_whole[n], w["kernel"][n].rearrange("h m d -> m h d")).then_inc(weights_in, 16)
            sp.dma_start(wv[:], w["kernel"][2].rearrange("h m d -> m h d")).then_inc(weights_in, 16)
            by_head = w["WO"][0].rearrange("(d p j) m -> j d p m", p=PAIRS, j=2)
            for j in range(2):
                sp.dma_start(wo[D * j:D * (j + 1), :, :], by_head[j]).then_inc(weights_in, 16)

            def max_row(pair, step):
                sp.wait_ge(maxT_done, pair + 1)
                sp.dma_start(q_am[D:D + 1, step % SLOTS, :, :].bitcast(F32),
                             maxT[:, step % 2, :].bitcast(F32)).then_inc(maxrow_in[step % 2], 16)

            max_row(0, 0)

            def iteration(i, parity, kind):
                for step in range(PAIRS if kind != "drain" else 0):
                    if moves_maxima(kind, step):
                        max_row(i * PAIRS + step + 1, step + 1)

            over_sequences(sp, iteration)

        @block.gpsimd
        def _(pool):
            pool.memset(ones[:], 1.0).then_inc(consts, 1)
            pool.wait_ge(consts, 1)
            pool.memset(k_b1[D:D + 1, :, :, :].bitcast(F32), -1.0).then_inc(consts, 1)
            pool.wait_ge(consts, 2)
            norms.pool_part(pool, 0)
            norms.pool_part(pool, 1)

            def sums(pair, step, i, kind):
                for h in range(2):
                    pool.wait_ge(exp_done, (pair * 2 + h + 1) * TILES)
                    if not (isinstance(pair, int) and pair == 0 and h == 0):
                        pool.wait_ge(part_done, pair * 2 + h)
                    if h == 0 and normalises(kind, step):
                        pool.wait_ge(misc_full, misc.at((step, "sum"), i, kind) + 1)
                    p = probs[:, step % 2, h, :]
                    part = part_sums[:, step % 2, h, :]
                    pool.tensor_tensor(part, p[:, 0:SEQ], p[:, SEQ:2 * SEQ], ALU.add).then_inc(half_done, 1)
                    pool.wait_ge(half_done, pair * 4 + 2 * h + 1)
                    pool.tensor_tensor(part, part, p[:, 2 * SEQ:3 * SEQ], ALU.add).then_inc(half_done, 1)
                    pool.wait_ge(half_done, pair * 4 + 2 * h + 2)
                    pool.tensor_tensor(part, part, p[:, 3 * SEQ:4 * SEQ], ALU.add).then_inc(part_done, 1)

            def iteration(i, parity, kind):
                for step in range(PAIRS if kind != "drain" else 0):
                    sums(i * PAIRS + step, step, i, kind)

            over_sequences(pool, iteration)

        @block.scalar
        def _(act):
            def copy_xnT(use):
                act.wait_ge(proj_full, use + 1)
                act.activation(xnT_part[:, 0, :], ps_proj[:], ACT.Copy).then_inc(xa_done, 1)
                act.activation(xnT[:], ps_proj[:], ACT.Copy).then_inc(xa_done, 1)

            def copy_v(c, use):
                act.wait_ge(proj_full, use + 1)
                act.activation(v[:, c // 2, SEQ * (c % 2):SEQ * (c % 2 + 1)], ps_proj[:],
                               ACT.Copy).then_inc(proj_free, 1)

            def first_parts(n, slot, pair, use):
                act.wait_ge(proj_full, use + 1)
                first = q_am if n == "q" else k_aa
                for h in range(2):
                    act.activation(first[0:D, slot, h, :], ps_proj[D * h:D * (h + 1), :], ACT.Copy)\
                        .then_inc(qa_done if n == "q" else ka_done, 1)

            def copy_first_parts(n, slot, pair):
                act.wait_ge(qa_done if n == "q" else ka_done, 2 * (pair + 1))
                first, copy = (q_am, q_ab) if n == "q" else (k_aa, k_aa)
                rows = slice(0, D) if n == "q" else slice(D, P)
                for h in range(2):
                    last = act.activation(copy[rows, slot, h, :], first[0:D, slot, h, :].bitcast(F32), ACT.Copy)
                last.then_inc(copied, 1)

            def exponentials(pair, step, j):
                h, kt = j // TILES, j % TILES
                act.wait_ge(exp_full, pair * 2 * TILES + j + 1)
                if j == 0 and not (isinstance(pair, int) and pair < 2):
                    act.wait_ge(part_done, 2 * (pair - 1))
                    act.wait_ge(pv_full, pair - 1)
                act.activation(probs[:, step % 2, h, SEQ * kt:SEQ * (kt + 1)], ps_exp[j % 3],
                               ACT.Exp, scale=SCALE).then_inc(exp_done, 1)

            act.wait_ge(weights_in, n_loads * 16)
            for n in range(2):
                act.activation(w_part["qk"[n]][:, 0], w_whole[n], ACT.Copy).then_inc(w_first_done, 1)
            copy_xnT(proj.at("xnT"))
            for c in range(0, 2 * TILES, 2):
                copy_v(c, proj.at(f"v{c}"))
            for p in range(PROJ_LEAD):
                for n in "qk":
                    first_parts(n, p, p, proj.at((p, n)))
                    copy_first_parts(n, p, p)

            def iteration(i, parity, kind):
                for step in range(PAIRS if kind != "drain" else 2):
                    pair = i * PAIRS + step
                    nxt = kind in ("first", "middle")
                    for u in range(4):
                        if kind != "drain":
                            exponentials(pair, step, 2 * u)
                        if u == 0 and nxt and step == 5:
                            copy_xnT(proj.at((step, "xnT"), i, kind))
                        if kind != "drain":
                            exponentials(pair, step, 2 * u + 1)
                        if u in proj_at(step) and projects(kind, step):
                            n = proj_at(step)[u]
                            first_parts(n, (step + PROJ_LEAD) % SLOTS, pair + PROJ_LEAD, proj.at((step, n), i, kind))
                        if u - 1 in proj_at(step) and projects(kind, step):
                            copy_first_parts(proj_at(step)[u - 1], (step + PROJ_LEAD) % SLOTS, pair + PROJ_LEAD)
                        if u == 0 and normalises(kind, step):
                            act.wait_ge(misc_full, misc.at((step, "sum"), i, kind) + 1)
                            act.activation(sumT[:], ps_misc[:], ACT.Copy).then_inc(misc_free, 1)
                        for c in v_uses(kind, step, u):
                            copy_v(c, proj.at((step, f"v{c}"), i, kind))
                    if weighs(kind, step):
                        act.wait_ge(pv_full, pair)
                        if not (kind == "first" and step <= 1):
                            act.wait_ge(normed_done, pair - 1)
                        act.activation(outT[:], ps_pv[:], ACT.Copy).then_inc(outT_done, 1)

            over_sequences(act, iteration)

        @block.vector
        def _(dve):
            norms.vector_part(dve, 0)

            def norm_apply(seq):
                dve.wait_ge(norms.rstd_done, 1 if isinstance(seq, int) and seq == 0 else 2)
                for t in range(TILES):
                    n = seq * TILES + t
                    dve.tensor_scalar(xn[:, t, :], x[:, n, :], norms.mean_var[:, n, 0:1],
                                      norms.rstd[:, bass.ds(n, 1)], ALU.subtract, ALU.mult).then_inc(xn_done, 1)

            def second_xnT(seq):
                dve.wait_ge(xa_done, 2 * (seq + 1))
                dve.tensor_tensor(xnT_part[:, 1, :], ps_proj[:], xnT_part[:, 0, :].bitcast(F32),
                                  ALU.subtract).then_inc(proj_free, 1)

            def second_part(n, slot, pair, h):
                dve.wait_ge(qa_done if n == "q" else ka_done, 2 * pair + h + 1)
                first = q_am if n == "q" else k_aa
                second = q_ab[D:P, slot, h, :] if n == "q" else k_b1[0:D, slot, h, :]
                last = dve.tensor_tensor(second, ps_proj[D * h:D * (h + 1), :],
                                         first[0:D, slot, h, :].bitcast(F32), ALU.subtract)
                if h == 1:
                    last.then_inc(proj_free, 1)

            def maximum(pair, step, unit):
                dve.wait_ge(max_full, pair * 8 + unit + 1)
                dve.tensor_reduce(rowmax[:, step % 2, unit:unit + 1], ps_max[unit % 2], AX.X, ALU.max)\
                    .then_inc(max_done, 1)

            def max_part(i, step, use):
                pair = i * PAIRS + step
                dve.wait_ge(misc_full, use + 1)
                if not (isinstance(pair, int) and pair < 2):
                    dve.wait_ge(maxrow_in[step % 2], 16 * moves(i, step - 2))
                dve.tensor_copy(maxT[:, step % 2, :], ps_misc[0:2 * TILES, 0:P]).then_inc(maxT_done, 1)
                dve.wait_ge(maxT_done, pair + 1)
                dve.sem_inc(misc_free, 1)

            norm_apply(0)
            norms.vector_part(dve, 1)
            for n in range(2):
                dve.wait_ge(w_first_done, n + 1)
                dve.tensor_tensor(w_part["qk"[n]][:, 1], w_whole[n], w_part["qk"[n]][:, 0].bitcast(F32),
                                  ALU.subtract).then_inc(w_parts_done, 1)
            second_xnT(0)
            for p in range(PROJ_LEAD):
                for n in "qk":
                    for h in range(2):
                        second_part(n, p, p, h)
            for p in range(MAX_LEAD):
                for unit in range(2 * TILES):
                    maximum(p, p, unit)
            max_part(0, 0, misc.at("max"))

            def iteration(i, parity, kind):
                for step in range(PAIRS if kind != "drain" else 2):
                    pair = i * PAIRS + step
                    for u in range(4):
                        if maximises(kind, step):
                            maximum(pair + MAX_LEAD, step + MAX_LEAD, 2 * u)
                        if u == 1 and moves_maxima(kind, step):
                            max_part(i, step + 1, misc.at((step, "max"), i, kind))
                        if u - 1 in proj_at(step) and projects(kind, step):
                            second_part(proj_at(step)[u - 1], (step + PROJ_LEAD) % SLOTS, pair + PROJ_LEAD, 1)
                        if u == 0 and step == 5 and kind in ("first", "middle"):
                            second_xnT(i + 1)
                        if maximises(kind, step):
                            maximum(pair + MAX_LEAD, step + MAX_LEAD, 2 * u + 1)
                        if u in proj_at(step) and projects(kind, step):
                            second_part(proj_at(step)[u], (step + PROJ_LEAD) % SLOTS, pair + PROJ_LEAD, 0)
                        if u == 1 and normalises(kind, step):
                            dve.wait_ge(misc_full, misc.at((step, "sumT"), i, kind) + 1)
                            sums = ps_misc[:].rearrange("p (t j c) -> p t j c", t=TILES, j=2)
                            dve.reciprocal(rsum[:], sums[:, :, :, 0]).then_inc(rsum_done, 1)
                            dve.wait_ge(rsum_done, pair - 1)
                            dve.sem_inc(misc_free, 1)
                        if u == 2 and normalises(kind, step):
                            dve.wait_ge(misc_full, misc.at((step, "recip"), i, kind) + 1)
                            dve.wait_ge(outT_done, pair - 1)
                            dve.tensor_tensor(normed[:, (step - 2) % PAIRS, :], ps_misc[:],
                                              outT[:], ALU.mult).then_inc(normed_done, 1)
                            dve.wait_ge(normed_done, pair - 1)
                            dve.sem_inc(misc_free, 1)
                    if step == 1 and kind != "first":
                        dve.wait_ge(misc_full, misc.at("y", i, kind) + 1)
                        rows = x[:, bass.ds((i - 1) * TILES, TILES), :]
                        dve.tensor_tensor(rows, rows, ps_misc[:].rearrange("p (t d) -> p t d", t=TILES),
                                          ALU.add).then_inc(misc_free, 1)
                    if step == 4 and kind in ("first", "middle"):
                        norm_apply(i + 1)

            over_sequences(dve, iteration)

        @block.tensor
        def _(pe):
            def wait_free(sem, use):
                if not (isinstance(use, int) and use == 0):
                    pe.wait_ge(sem, use)

            def transposed_norm(seq, use):
                pe.wait_ge(xn_done, (seq + 1) * TILES)
                wait_free(proj_free, use)
                for t in range(TILES):
                    last = pe.transpose(ps_proj[:, P * t:P * (t + 1)], xn[:, t, :], ident[:])
                last.then_inc(proj_full, 1)

            def values(c, use):
                wait_free(proj_free, use)
                kt, half = c // 2, c % 2
                rhs = wv[:, HEADS // 2 * half:HEADS // 2 * (half + 1), :].rearrange("p h d -> p (h d)")
                pe.matmul(ps_proj[:], xnT[:, P * kt:P * (kt + 1)], rhs, start=True, stop=True).then_inc(proj_full, 1)

            def projection(n, pair, use):
                wait_free(proj_free, use)
                heads = slice(2 * pair, 2 * pair + 2)
                for wp, xp in ((0, 0), (0, 1), (1, 0)):
                    last = pe.matmul(ps_proj[:], w_part[n][:, wp, heads, :].rearrange("p h d -> p (h d)"),
                                     xnT_part[:, xp, :], start=(wp + xp == 0), stop=(wp == 1))
                last.then_inc(proj_full, 1)

            def scores_for_max(pair, slot, unit):
                h, t = unit // TILES, unit % TILES
                index = pair * 8 + unit
                if not (isinstance(index, int) and index < 2):
                    pe.wait_ge(max_done, index - 1)
                pe.matmul(ps_max[unit % 2], q_ab[:, slot, h, P * t:P * (t + 1)], k_aa[:, slot, h, :],
                          start=True, stop=True).then_inc(max_full, 1)

            def scores_for_exp(i, step, slot, j):
                pair = i * PAIRS + step
                h, keys = j // TILES, slice(P * (j % TILES), P * (j % TILES + 1))
                if j == 0:
                    pe.wait_ge(maxrow_in[step % 2], 16 * moves(i, step))
                before = j - 3 if j >= 3 else {0: 6, 1: 7, 2: 5}[j] - 2 * TILES
                if j >= 3 or not (isinstance(pair, int) and pair == 0):
                    pe.wait_ge(exp_done, pair * 2 * TILES + before + 1)
                bank = ps_exp[j % 3]
                pe.matmul(bank, k_aa[:, slot, h, keys], q_ab[:, slot, h, :], start=True, stop=False)
                pe.matmul(bank, k_b1[:, slot, h, keys], q_am[:, slot, h, :], start=False, stop=True)\
                    .then_inc(exp_full, 1)

            def weigh_values(pair, step, kt):
                for j in range(2):
                    head = 2 * step + j
                    last = pe.matmul(ps_pv[D * j:D * (j + 1), :], v[:, kt, D * head:D * (head + 1)],
                                     probs[:, step % 2, j, SEQ * kt:SEQ * (kt + 1)],
                                     start=(kt == 0), stop=(kt == TILES - 1))
                if kt == TILES - 1:
                    last.then_inc(pv_full, 1)

            def output_projection(use):
                wait_free(misc_free, use)
                for t in range(TILES):
                    for p in range(PAIRS):
                        last = pe.matmul(ps_misc[:, P * t:P * (t + 1)], normed[:, p, P * t:P * (t + 1)], wo[:, p, :],
                                         start=(p == 0), stop=(p == PAIRS - 1))
                last.then_inc(misc_full, 1)

            pe.wait_ge(weights_in, n_loads * 16)
            pe.wait_ge(consts, 2)
            transposed_norm(0, proj.at("xnT"))
            for c in range(0, 2 * TILES, 2):
                values(c, proj.at(f"v{c}"))
            pe.wait_ge(w_parts_done, 2)
            for p in range(PROJ_LEAD):
                for n in "qk":
                    projection(n, p, proj.at((p, n)))
            pe.wait_ge(proj_free, proj.at((MAX_LEAD - 1, "k")) + 1)
            pe.wait_ge(copied, 2 * MAX_LEAD)
            for p in range(MAX_LEAD):
                for unit in range(2 * TILES):
                    scores_for_max(p, p, unit)
            pe.wait_ge(max_done, 2 * TILES)
            pe.transpose(ps_misc[0:2 * TILES, 0:P], rowmax[:, 0, :], ident[:]).then_inc(misc_full, 1)

            def iteration(i, parity, kind):
                nxt = kind in ("first", "middle")
                for step in range(PAIRS if kind != "drain" else 2):
                    pair = i * PAIRS + step
                    if maximises(kind, step):
                        pe.wait_ge(proj_free, proj.before(step, i, kind))
                        pe.wait_ge(copied, 2 * (pair + MAX_LEAD + 1))
                    for u in range(4):
                        slot = (step + MAX_LEAD) % SLOTS
                        if maximises(kind, step):
                            scores_for_max(pair + MAX_LEAD, slot, 2 * u)
                        if kind != "drain":
                            scores_for_exp(i, step, step % SLOTS, 2 * u)
                        if u == 1 and moves_maxima(kind, step):
                            pe.wait_ge(max_done, (pair + 2) * 2 * TILES)
                            wait_free(misc_free, misc.at((step, "max"), i, kind))
                            pe.transpose(ps_misc[0:2 * TILES, 0:P], rowmax[:, (step + 1) % 2, :], ident[:])\
                                .then_inc(misc_full, 1)
                        if u == 0 and nxt and step == 5:
                            transposed_norm(i + 1, proj.at((step, "xnT"), i, kind))
                        if maximises(kind, step):
                            scores_for_max(pair + MAX_LEAD, slot, 2 * u + 1)
                        if kind != "drain":
                            scores_for_exp(i, step, step % SLOTS, 2 * u + 1)
                        if u in proj_at(step) and projects(kind, step):
                            n = proj_at(step)[u]
                            projection(n, (step + PROJ_LEAD) % PAIRS, proj.at((step, n), i, kind))
                        if weighs(kind, step):
                            if u == 0:
                                pe.wait_ge(exp_done, pair * 2 * TILES)
                                if not (kind == "first" and step == 1):
                                    pe.wait_ge(outT_done, pair - 1)
                            weigh_values(pair - 1, (step - 1) % PAIRS, u)
                        if normalises(kind, step):
                            if u == 0:
                                pe.wait_ge(part_done, 2 * (pair - 1))
                                wait_free(misc_free, misc.at((step, "sum"), i, kind))
                                for j in range(2):
                                    last = pe.matmul(ps_misc[D * j:D * (j + 1), :], ones[:],
                                                     part_sums[:, step % 2, j, :], start=True, stop=True)
                                last.then_inc(misc_full, 1)
                            if u == 1:
                                wait_free(misc_free, misc.at((step, "sumT"), i, kind))
                                for t in range(TILES):
                                    last = pe.transpose(ps_misc[:, P * t:P * (t + 1)], sumT[:, P * t:P * (t + 1)],
                                                        ident[:])
                                last.then_inc(misc_full, 1)
                            if u == 2:
                                wait_free(misc_free, misc.at((step, "recip"), i, kind))
                                pe.wait_ge(rsum_done, pair - 1)
                                for t in range(TILES):
                                    for j in range(2):
                                        last = pe.matmul(ps_misc[D * j:D * (j + 1), P * t:P * (t + 1)],
                                                         rsum[:, t, j:j + 1].to_broadcast([P, D]), ident[:],
                                                         start=True, stop=True)
                                last.then_inc(misc_full, 1)
                        for c in v_uses(kind, step, u):
                            values(c, proj.at((step, f"v{c}"), i, kind))
                    if step == 1 and kind != "first":
                        output_projection(misc.at("y", i, kind))

            over_sequences(pe, iteration)


def build(nc, t, out, stages=("a0",)):
    with ExitStack() as ctx:
        x = ctx.enter_context(nc.sbuf_tensor("x", [P, SEQS * TILES, P], F32))
        ident = ctx.enter_context(nc.sbuf_tensor("ident", [P, P], F32))
        banks = ctx.enter_context(nc.psum_tensor("banks", [P, 8 * SEQ], F32))
        x_dram = t["L0_attn_a_x"].rearrange("b (t p) d -> p (b t) d", p=P)
        out_dram = out.rearrange("b (t p) d -> p (b t) d", p=P)

        D = P // HEADS

        def separate(prefix, out_major):
            w = {n: t[f"{prefix}W{n}"] for n in "qkvo"}
            w.update({b: t[prefix + b] for b in ("bv", "bo")})
            w.update({b: t[prefix + b].rearrange("(h d u) -> d h u", d=D, u=1) for b in ("bq", "bk")})
            return {**w, "out_major": out_major}

        def fused(prefix):
            wqkv = t[prefix + "W_qkv"].rearrange("(h c d) i -> c h d i", c=3, d=D)
            bqkv = t[prefix + "b_qkv"]
            by_dim = bqkv.rearrange("(h c d u) -> c d h u", c=3, d=D, u=1)
            return {"q": wqkv[0], "k": wqkv[1], "v": wqkv[2], "o": t[prefix + "W_out"],
                    "bq": by_dim[0], "bk": by_dim[1], "bv": bqkv.rearrange("(h c d) -> c h d", c=3, d=D)[2],
                    "bo": t[prefix + "b_out"], "out_major": True}

        def narrow_weights(name, w, within):
            return NarrowWeights(nc, within, name, w, w["out_major"])

        attn1_weights = narrow_weights("attn1_w", separate("L1_attn_a_", True), ctx)
        ffn_ctx = ctx.enter_context(ExitStack())
        ffn_weights = FfnWeights(nc, ffn_ctx, "ffn_w", {n: t["L0_ffn_" + n] for n in (
            "Wg", "bg", "Wu", "bu", "Wd", "bd", "Wq", "keys", "down_embed", "up_embed")})
        patch_ctx = ctx.enter_context(ExitStack())
        patch_weights = narrow_weights("patch_w", separate("L0_attn_a_", False), patch_ctx)

        def load_later(sp):
            ffn_weights.load(sp)
            attn1_weights.load(sp)

        rest_of_x = ctx.enter_context(nc.semaphore("rest_of_x"))

        with nc.semaphore("x_in") as x_in, nc.semaphore("ident_done") as ident_done, nc.Block() as block:
            @block.sync
            def _(sp):
                sp.dma_start(x[:, 0:TILES, :], x_dram[:, 0:TILES, :]).then_inc(x_in, 16)
                patch_weights.load(sp)
                sp.dma_start(x[:, TILES:, :], x_dram[:, TILES:, :]).then_inc(rest_of_x, 16)
                sp.wait_ge(x_in, 16)

            @block.gpsimd
            def _(pool):
                pool.memset(ident[:], 0.0).then_inc(ident_done, 1)
                pool.wait_ge(ident_done, 1)
                pool.affine_select(out=ident[:], in_=ident[:], compare_op=ALU.not_equal, fill=1.0, base=0,
                                   pattern=[[-1, P]], channel_multiplier=1).then_inc(ident_done, 1)
                ffn_weights.clear_keys(pool)
                pool.wait_ge(ident_done, 2)

        for stage in stages:
            if stage == "a0":
                narrow_attention(nc, "patch", x, ident, banks, patch_weights, True, load_later,
                                 rest_of_x)
                patch_ctx.close()
            elif stage == "f0":
                product_key_ffn(nc, "ffn0", x, ident, banks, ffn_weights, True)
                ffn_weights.raw_ctx.close()
            elif stage == "f1":
                product_key_ffn(nc, "ffn1", x, ident, banks, ffn_weights, False)
                ffn_ctx.close()
            elif stage == "a1":
                attn2_weights = narrow_weights("attn2_w", fused("L1_attn_b_"), ctx)
                narrow_attention(nc, "attn1", x, ident, banks, attn1_weights, False, attn2_weights.load)
            elif stage == "b0":
                wide_attention(nc, "wide", x, ident, banks, {n: t["L0_attn_b_" + n] for n in ("kernel", "WO")})
            elif stage in ("l0", "l1"):
                if stage == "l0":
                    folded = ctx.enter_context(nc.sbuf_tensor("folded", [P, SEQS, P], F32))
                    folded_bias = ctx.enter_context(nc.sbuf_tensor("folded_bias", [P, SEQS, P], F32))
                linear_ffn(nc, "lin" + stage[1], x, ident, banks, {n: t["L1_ffn_" + n] for n in ("W1", "b1", "W2", "b2")},
                           folded, folded_bias, stage == "l0", out_dram if stage == "l1" else None)
            elif stage == "b1":
                narrow_attention(nc, "attn2", x, ident, banks, attn2_weights, False, lambda sp: None)


_INS = ['L0_attn_a_x', 'L0_attn_a_Wq', 'L0_attn_a_bq', 'L0_attn_a_Wk', 'L0_attn_a_bk', 'L0_attn_a_Wv',
        'L0_attn_a_bv', 'L0_attn_a_Wo', 'L0_attn_a_bo', 'L0_attn_b_kernel', 'L0_attn_b_WO',
        'L0_ffn_Wg', 'L0_ffn_bg', 'L0_ffn_Wu', 'L0_ffn_bu', 'L0_ffn_Wd', 'L0_ffn_bd', 'L0_ffn_Wq',
        'L0_ffn_keys', 'L0_ffn_down_embed', 'L0_ffn_up_embed', 'L1_attn_a_Wq', 'L1_attn_a_bq',
        'L1_attn_a_Wk', 'L1_attn_a_bk', 'L1_attn_a_Wv', 'L1_attn_a_bv', 'L1_attn_a_Wo', 'L1_attn_a_bo',
        'L1_attn_b_W_qkv', 'L1_attn_b_b_qkv', 'L1_attn_b_W_out', 'L1_attn_b_b_out', 'L1_ffn_W1',
        'L1_ffn_b1', 'L1_ffn_W2', 'L1_ffn_b2']
_STAGES = ('a0', 'f0', 'b0', 'f1', 'a1', 'l0', 'b1', 'l1')


def kernel(**inputs):
    import numpy as _np
    import concourse.bacc as _bacc
    from concourse import mybir as _mybir
    from concourse.bass_utils import run_bass_kernel_spmd as _run

    nc = _bacc.Bacc("TRN2", target_bir_lowering=False, num_devices=1)
    arrays, t = {}, {}
    for name in _INS:
        a = _np.ascontiguousarray(inputs[name])
        arrays[f"in_{name}_dram"] = a
        t[name] = nc.dram_tensor(f"in_{name}_dram", a.shape, _mybir.dt.from_np(a.dtype), kind="ExternalInput").ap()
    out = nc.dram_tensor("out_0_dram", (SEQS, SEQ, P), _mybir.dt.float32, kind="ExternalOutput").ap()
    build(nc, t, out, _STAGES)
    r = _run(nc, [arrays], core_ids=[0])
    return r.results[0]["out_0_dram"]
```
